# Optimizing a Trainium2 kernel written in Bass

```python
import numpy as np
import jax
import jax.numpy as jnp

def _softmax(x, axis=-1):
    return jax.nn.softmax(x, axis=axis)

def _gelu(x):
    return jax.nn.gelu(x, approximate=True)

def _silu(x):
    return jax.nn.silu(x)

def _sigmoid(x):
    return jax.nn.sigmoid(x)

def _layernorm(x, axis=-1, eps=1e-05):
    m = jnp.mean(x, axis=axis, keepdims=True)
    v = jnp.var(x, axis=axis, keepdims=True)
    return (x - m) / jnp.sqrt(v + eps)

def _scatter_add(tgt, idx, src, axis=0):
    return tgt.at[idx].add(src)

def _segment_sum(src, seg, n):
    return jax.ops.segment_sum(src, seg, n)
kernel_name = 'mk_dlrm_tower_d1_rec_r8_8f3510'

def setup_inputs(seed: int=0):
    np.random.seed(seed)
    _w = jnp.asarray

    def _rec_inputs():
        import jax
        import jax.numpy as jnp
        _tk = jax.random.key(seed)
        dense_ctx = jax.random.normal(jax.random.fold_in(_tk, 190), (1024, 16), jnp.float32)
        ids = jnp.stack([jax.random.randint(jax.random.fold_in(_tk, 200 + f), (1024,), 0, v, jnp.int32) for f, v in enumerate([1000, 125000, 125000, 12500, 12500, 1000, 1000, 1250, 12500, 12500, 12500, 1000, 12500, 1000, 1000, 12500, 125000, 1250, 125000, 1250, 1250, 12500, 1000, 12500, 1000, 1250, 125000, 1000, 125000, 1250, 1250, 1250])], axis=1)
        tbl_0 = 0.05 * jax.random.normal(jax.random.fold_in(_tk, 500 + 0), (1000, 32), jnp.float32)
        tbl_1 = 0.05 * jax.random.normal(jax.random.fold_in(_tk, 500 + 1), (125000, 32), jnp.float32)
        tbl_2 = 0.05 * jax.random.normal(jax.random.fold_in(_tk, 500 + 2), (125000, 32), jnp.float32)
        tbl_3 = 0.05 * jax.random.normal(jax.random.fold_in(_tk, 500 + 3), (12500, 32), jnp.float32)
        tbl_4 = 0.05 * jax.random.normal(jax.random.fold_in(_tk, 500 + 4), (12500, 32), jnp.float32)
        tbl_5 = 0.05 * jax.random.normal(jax.random.fold_in(_tk, 500 + 5), (1000, 32), jnp.float32)
        tbl_6 = 0.05 * jax.random.normal(jax.random.fold_in(_tk, 500 + 6), (1000, 32), jnp.float32)
        tbl_7 = 0.05 * jax.random.normal(jax.random.fold_in(_tk, 500 + 7), (1250, 32), jnp.float32)
        tbl_8 = 0.05 * jax.random.normal(jax.random.fold_in(_tk, 500 + 8), (12500, 32), jnp.float32)
        tbl_9 = 0.05 * jax.random.normal(jax.random.fold_in(_tk, 500 + 9), (12500, 32), jnp.float32)
        tbl_10 = 0.05 * jax.random.normal(jax.random.fold_in(_tk, 500 + 10), (12500, 32), jnp.float32)
        tbl_11 = 0.05 * jax.random.normal(jax.random.fold_in(_tk, 500 + 11), (1000, 32), jnp.float32)
        tbl_12 = 0.05 * jax.random.normal(jax.random.fold_in(_tk, 500 + 12), (12500, 32), jnp.float32)
        tbl_13 = 0.05 * jax.random.normal(jax.random.fold_in(_tk, 500 + 13), (1000, 32), jnp.float32)
        tbl_14 = 0.05 * jax.random.normal(jax.random.fold_in(_tk, 500 + 14), (1000, 32), jnp.float32)
        tbl_15 = 0.05 * jax.random.normal(jax.random.fold_in(_tk, 500 + 15), (12500, 32), jnp.float32)
        tbl_16 = 0.05 * jax.random.normal(jax.random.fold_in(_tk, 500 + 16), (125000, 32), jnp.float32)
        tbl_17 = 0.05 * jax.random.normal(jax.random.fold_in(_tk, 500 + 17), (1250, 32), jnp.float32)
        tbl_18 = 0.05 * jax.random.normal(jax.random.fold_in(_tk, 500 + 18), (125000, 32), jnp.float32)
        tbl_19 = 0.05 * jax.random.normal(jax.random.fold_in(_tk, 500 + 19), (1250, 32), jnp.float32)
        tbl_20 = 0.05 * jax.random.normal(jax.random.fold_in(_tk, 500 + 20), (1250, 32), jnp.float32)
        tbl_21 = 0.05 * jax.random.normal(jax.random.fold_in(_tk, 500 + 21), (12500, 32), jnp.float32)
        tbl_22 = 0.05 * jax.random.normal(jax.random.fold_in(_tk, 500 + 22), (1000, 32), jnp.float32)
        tbl_23 = 0.05 * jax.random.normal(jax.random.fold_in(_tk, 500 + 23), (12500, 32), jnp.float32)
        tbl_24 = 0.05 * jax.random.normal(jax.random.fold_in(_tk, 500 + 24), (1000, 32), jnp.float32)
        tbl_25 = 0.05 * jax.random.normal(jax.random.fold_in(_tk, 500 + 25), (1250, 32), jnp.float32)
        tbl_26 = 0.05 * jax.random.normal(jax.random.fold_in(_tk, 500 + 26), (125000, 32), jnp.float32)
        tbl_27 = 0.05 * jax.random.normal(jax.random.fold_in(_tk, 500 + 27), (1000, 32), jnp.float32)
        tbl_28 = 0.05 * jax.random.normal(jax.random.fold_in(_tk, 500 + 28), (125000, 32), jnp.float32)
        tbl_29 = 0.05 * jax.random.normal(jax.random.fold_in(_tk, 500 + 29), (1250, 32), jnp.float32)
        tbl_30 = 0.05 * jax.random.normal(jax.random.fold_in(_tk, 500 + 30), (1250, 32), jnp.float32)
        tbl_31 = 0.05 * jax.random.normal(jax.random.fold_in(_tk, 500 + 31), (1250, 32), jnp.float32)
        _rk = jax.random.fold_in(_tk, 7)
        W_top1 = 0.0606339 * jax.random.normal(jax.random.fold_in(_tk, 801), (272, 512), jnp.float32)
        W_top2 = 0.0441942 * jax.random.normal(jax.random.fold_in(_tk, 802), (512, 256), jnp.float32)
        W_top3 = 0.0625 * jax.random.normal(jax.random.fold_in(_tk, 803), (256, 1), jnp.float32)
        b_top1 = jnp.zeros((512,), jnp.float32)
        b_top2 = jnp.zeros((256,), jnp.float32)
        return (dense_ctx, ids, tbl_0, tbl_1, tbl_2, tbl_3, tbl_4, tbl_5, tbl_6, tbl_7, tbl_8, tbl_9, tbl_10, tbl_11, tbl_12, tbl_13, tbl_14, tbl_15, tbl_16, tbl_17, tbl_18, tbl_19, tbl_20, tbl_21, tbl_22, tbl_23, tbl_24, tbl_25, tbl_26, tbl_27, tbl_28, tbl_29, tbl_30, tbl_31, W_top1, b_top1, W_top2, b_top2, W_top3)
    dense_ctx, ids, tbl_0, tbl_1, tbl_2, tbl_3, tbl_4, tbl_5, tbl_6, tbl_7, tbl_8, tbl_9, tbl_10, tbl_11, tbl_12, tbl_13, tbl_14, tbl_15, tbl_16, tbl_17, tbl_18, tbl_19, tbl_20, tbl_21, tbl_22, tbl_23, tbl_24, tbl_25, tbl_26, tbl_27, tbl_28, tbl_29, tbl_30, tbl_31, W_top1, b_top1, W_top2, b_top2, W_top3 = _rec_inputs()

    def _L0_rec_setup():
        import jax, jax.numpy as jnp
        import numpy as np
        B, F, D = (512, 32, 32)
        LAYER_SIZE = [128, 128]

        def _cin_forward(inputs, filters):
            x0 = inputs
            prev = inputs
            outs = []
            for W in filters:
                z = jnp.einsum('bhd,bmd->bhmd', x0, prev)
                b, h, m, d = z.shape
                z = z.reshape(b, h * m, d)
                cur = jnp.einsum('bpd,pn->bnd', z, W[0])
                cur = jax.nn.relu(cur)
                prev = cur
                outs.append(cur)
            result = jnp.concatenate(outs, axis=1)
            return jnp.sum(result, axis=-1)
        key = jax.random.key(seed)
        k1, k2, k3 = jax.random.split(key, 3)
        inputs = jax.random.normal(k1, (B, F, D), dtype=jnp.float32)
        field_nums = [F] + LAYER_SIZE
        filter_0 = jax.random.normal(k2, (1, field_nums[0] * field_nums[0], field_nums[1]), dtype=jnp.float32) * 0.05
        filter_1 = jax.random.normal(k3, (1, field_nums[0] * field_nums[1], field_nums[2]), dtype=jnp.float32) * 0.05
        return {'inputs': inputs, 'filter_0': filter_0, 'filter_1': filter_1}
    _L0_rec_all = _L0_rec_setup()
    _L0_rec_in = {k: v for k, v in _L0_rec_all.items() if k in ('filter_0', 'filter_1')}
    del _L0_rec_all
    return {'dense_ctx': dense_ctx, 'ids': ids, 'tbl_0': tbl_0, 'tbl_1': tbl_1, 'tbl_2': tbl_2, 'tbl_3': tbl_3, 'tbl_4': tbl_4, 'tbl_5': tbl_5, 'tbl_6': tbl_6, 'tbl_7': tbl_7, 'tbl_8': tbl_8, 'tbl_9': tbl_9, 'tbl_10': tbl_10, 'tbl_11': tbl_11, 'tbl_12': tbl_12, 'tbl_13': tbl_13, 'tbl_14': tbl_14, 'tbl_15': tbl_15, 'tbl_16': tbl_16, 'tbl_17': tbl_17, 'tbl_18': tbl_18, 'tbl_19': tbl_19, 'tbl_20': tbl_20, 'tbl_21': tbl_21, 'tbl_22': tbl_22, 'tbl_23': tbl_23, 'tbl_24': tbl_24, 'tbl_25': tbl_25, 'tbl_26': tbl_26, 'tbl_27': tbl_27, 'tbl_28': tbl_28, 'tbl_29': tbl_29, 'tbl_30': tbl_30, 'tbl_31': tbl_31, 'W_top1': W_top1, 'b_top1': b_top1, 'W_top2': W_top2, 'b_top2': b_top2, 'W_top3': W_top3, 'L0_rec_filter_0': _L0_rec_in['filter_0'], 'L0_rec_filter_1': _L0_rec_in['filter_1']}

def reference(dense_ctx, ids, tbl_0, tbl_1, tbl_2, tbl_3, tbl_4, tbl_5, tbl_6, tbl_7, tbl_8, tbl_9, tbl_10, tbl_11, tbl_12, tbl_13, tbl_14, tbl_15, tbl_16, tbl_17, tbl_18, tbl_19, tbl_20, tbl_21, tbl_22, tbl_23, tbl_24, tbl_25, tbl_26, tbl_27, tbl_28, tbl_29, tbl_30, tbl_31, W_top1, b_top1, W_top2, b_top2, W_top3, L0_rec_filter_0, L0_rec_filter_1):
    import jax
    import jax.numpy as jnp

    def _L0_rec_ref(inputs, filter_0, filter_1):
        import jax, jax.numpy as jnp
        import numpy as np
        B, F, D = (512, 32, 32)
        LAYER_SIZE = [128, 128]

        def _cin_forward(inputs, filters):
            x0 = inputs
            prev = inputs
            outs = []
            for W in filters:
                z = jnp.einsum('bhd,bmd->bhmd', x0, prev)
                b, h, m, d = z.shape
                z = z.reshape(b, h * m, d)
                cur = jnp.einsum('bpd,pn->bnd', z, W[0])
                cur = jax.nn.relu(cur)
                prev = cur
                outs.append(cur)
            result = jnp.concatenate(outs, axis=1)
            return jnp.sum(result, axis=-1)
        return _cin_forward(inputs, (filter_0, filter_1))
    e = jnp.stack([tbl_0[ids[:, 0]], tbl_1[ids[:, 1]], tbl_2[ids[:, 2]], tbl_3[ids[:, 3]], tbl_4[ids[:, 4]], tbl_5[ids[:, 5]], tbl_6[ids[:, 6]], tbl_7[ids[:, 7]], tbl_8[ids[:, 8]], tbl_9[ids[:, 9]], tbl_10[ids[:, 10]], tbl_11[ids[:, 11]], tbl_12[ids[:, 12]], tbl_13[ids[:, 13]], tbl_14[ids[:, 14]], tbl_15[ids[:, 15]], tbl_16[ids[:, 16]], tbl_17[ids[:, 17]], tbl_18[ids[:, 18]], tbl_19[ids[:, 19]], tbl_20[ids[:, 20]], tbl_21[ids[:, 21]], tbl_22[ids[:, 22]], tbl_23[ids[:, 23]], tbl_24[ids[:, 24]], tbl_25[ids[:, 25]], tbl_26[ids[:, 26]], tbl_27[ids[:, 27]], tbl_28[ids[:, 28]], tbl_29[ids[:, 29]], tbl_30[ids[:, 30]], tbl_31[ids[:, 31]]], axis=1)
    z = _L0_rec_ref(e, L0_rec_filter_0, L0_rec_filter_1)
    z = z.reshape(z.shape[0], -1)
    h = jnp.concatenate([z, dense_ctx], axis=1)
    h = jnp.maximum(h @ W_top1 + b_top1, 0.0)
    h = jnp.maximum(h @ W_top2 + b_top2, 0.0)
    y = h @ W_top3
    return y

_drawn_inputs = setup_inputs


def setup_inputs(seed=0):
    import zlib

    import numpy as np

    out = dict(_drawn_inputs(seed))
    spreads = {'b_top1': (0.0, 0.436), 'b_top2': (0.0, 0.416)}
    factors = {'tbl_0': 5.874,
     'tbl_1': 5.859,
     'tbl_2': 5.757,
     'tbl_3': 6.459,
     'tbl_4': 5.963,
     'tbl_5': 5.876,
     'tbl_6': 5.927,
     'tbl_7': 6.349,
     'tbl_8': 6.111,
     'tbl_9': 6.174,
     'tbl_10': 5.87,
     'tbl_11': 6.1,
     'tbl_12': 6.003,
     'tbl_13': 6.163,
     'tbl_14': 6.194,
     'tbl_15': 6.115,
     'tbl_16': 6.37,
     'tbl_17': 5.883,
     'tbl_18': 6.292,
     'tbl_19': 6.345,
     'tbl_20': 5.719,
     'tbl_21': 5.934,
     'tbl_22': 6.022,
     'tbl_23': 6.109,
     'tbl_24': 5.938,
     'tbl_25': 6.03,
     'tbl_26': 6.076,
     'tbl_27': 6.408,
     'tbl_28': 5.881,
     'tbl_29': 6.151,
     'tbl_30': 6.176,
     'tbl_31': 5.885,
     'L0_rec_filter_1': 8.0}
    for name, (base, spread) in spreads.items():
        noise = np.random.default_rng([zlib.crc32(name.encode()), seed]).standard_normal(out[name].shape)
        drawn = base * np.exp(spread * noise) if base else spread * noise
        out[name] = jnp.asarray(drawn.astype(out[name].dtype))
    for name, factor in factors.items():
        out[name] = (out[name] * factor).astype(out[name].dtype)
    return out
```

```python
from contextlib import ExitStack

import numpy as np

import concourse.bass as bass
from concourse import mybir

ALU = mybir.AluOpType
ACT = mybir.ActivationFunctionType
AX = mybir.AxisListType
F32 = mybir.dt.float32
F32R = mybir.dt.float32r
I32 = mybir.dt.int32

P = 128
B, F, D, N = 1024, 32, 32, 128
GROUPS = B // P
CPG = 8
DPC = D // CPG
COLS = DPC * P
CHUNKS = GROUPS * CPG
LAST = CHUNKS - 1
TILES0 = 4
DENSE, H1, H2 = 16, 512, 256

PAIRS = F // 2
HALF = PAIRS // 2
PER = 2 + PAIRS
HEAD = 2 + HALF
STEPS = CHUNKS * PER

AHEAD = 4
DELTA = 2
SPREADS, PRODS, HIS, LOS = 2, 4, 6, 4
DVE_SUBS = (1, 4, 6, 9, 12, 14, 17)


def place(s):
    if s < 2:
        return s
    if s < HEAD:
        return s + PER - HEAD
    k, j = divmod(s - HEAD, PER)
    return j + 2 if k == LAST else j


def decode(s):
    j = place(s)
    k = -1 if s < HEAD else (s - HEAD) // PER
    if j < 2:
        return 0, k + 1, j
    if j < 2 + HALF:
        return 1, k, j - 2 + HALF
    return 1, k + 1, j - 2 - HALF


def on_dve(s):
    return place(s) in DVE_SUBS


DVE_PER = len(DVE_SUBS)
POOL_PER = PER - DVE_PER
DVE_BEFORE = [0]
for _s in range(STEPS):
    DVE_BEFORE.append(DVE_BEFORE[-1] + on_dve(_s))


def dve_before(s):
    return DVE_BEFORE[s]


def pool_before(s):
    return s - DVE_BEFORE[s]


def last_step(chunk):
    return HEAD + PER * chunk + (1 if chunk < LAST else -1) + HALF


def build(nc, tables, ids, w0a, w0b, w1, consts, dense_t, wt1, wt1d, wt2, wt3, bt1, bt2, out):
    with ExitStack() as ctx:
        def sb(name, shape, dt=F32):
            return ctx.enter_context(nc.sbuf_tensor(name, shape, dt))

        def sem(name):
            return ctx.enter_context(nc.semaphore(name))

        spread = ctx.enter_context(nc.psum_tensor("spread", [P, SPREADS, 2, COLS], F32))
        acc1 = ctx.enter_context(nc.psum_tensor("acc1", [P, 2, COLS], F32))
        acc0 = ctx.enter_context(nc.psum_tensor("acc0", [P, COLS], F32))
        misc = ctx.enter_context(nc.psum_tensor("misc", [P, COLS], F32))

        prod = sb("prod", [P, PRODS, 2, COLS])
        hi = sb("hi", [P, HIS, 2, COLS], F32R)
        lo = sb("lo", [P, LOS, 2, COLS], F32R)

        f1h = sb("f1h", [P, F, N], F32R)
        f1l = sb("f1l", [P, F, N], F32R)
        f0h = sb("f0h", [P, TILES0, N], F32R)
        f0l = sb("f0l", [P, TILES0, N], F32R)
        f16 = sb("f16", [P, N], F32R)
        pick = sb("pick", [P, F, P], F32R)
        shift = sb("shift", [P, 6, P], F32R)
        ident = sb("ident", [P, P])

        ids_sb = sb("ids_sb", [P, GROUPS, F], I32)
        ids_now = sb("ids_now", [P, F], I32)
        rows = sb("rows", [P, F, D])
        emb = sb("emb", [P, 2 * CPG, DPC, 2 * F], F32R)
        stage = sb("stage", [P, DPC, 2, 2 * F])
        est = sb("est", [P, 2, COLS], F32R)
        e4 = sb("e4", [P, COLS])
        c0 = sb("c0", [P, 2, COLS])
        p16 = sb("p16", [P, COLS])
        x16 = sb("x16", [P, COLS], F32R)

        zacc = sb("zacc", [P, 2, GROUPS, COLS])
        zsum = sb("zsum", [P, 2, B])
        wt1_sb = sb("wt1_sb", [P, 2, H1])
        wt1d_sb = sb("wt1d_sb", [DENSE, H1])
        wt2_sb = sb("wt2_sb", [P, H1 // P, H2])
        wt3_sb = sb("wt3_sb", [P, H2 // P])
        bt1_sb = sb("bt1_sb", [P, H1 // P])
        bt2_sb = sb("bt2_sb", [P, H2 // P])
        dense_sb = sb("dense_sb", [DENSE, B])

        raw = zacc[:].rearrange("p a g c -> p (a g c)")
        w1_raw = raw[:, 0:F * N].rearrange("p (h n) -> p h n", n=N)
        at = F * N
        w0a_raw = raw[:, at:at + 5 * N].rearrange("p (t n) -> p t n", n=N)
        at += 5 * N
        w0b_raw = raw[:, at:at + 4 * N].rearrange("p (t n) -> p t n", n=N)
        at += 4 * N
        pick_raw = raw[:, at:at + F]
        at += F
        shift_raw = raw[:, at:at + 6 * P].rearrange("p (t n) -> p t n", n=P)
        ring = prod[:].rearrange("p a b c -> p (a b c)")
        h1 = ring[:, 0:4 * 512].rearrange("p (m c) -> p m c", c=512)
        h2 = ring[:, 4 * 512:6 * 512].rearrange("p (m c) -> p m c", c=512)
        y_sb = ring[0:1, 6 * 512:8 * 512]

        ids_in, f1_in, f0_in, const_in, tower_in = (
            sem(x) for x in ("ids_in", "f1_in", "f0_in", "const_in", "tower_in"))
        split_hi, f0_sum, split_lo, consts_ready, cleared = (
            sem(x) for x in ("split_hi", "f0_sum", "split_lo", "consts_ready", "cleared"))
        ids_ready, gathered, emb_hi, emb_ready = (
            sem(x) for x in ("ids_ready", "gathered", "emb_hi", "emb_ready"))
        staged, turned, est_ready, e4_spread, e4_ready = (
            sem(x) for x in ("staged", "turned", "est_ready", "e4_spread", "e4_ready"))
        spread_ready, prod_ready, hi_ready, lo_pool, lo_dve, step_done = (
            sem(x) for x in ("spread_ready", "prod_ready", "hi_ready", "lo_pool", "lo_dve", "step_done"))
        s16_spread, p16_ready, x16_hi, x16_ready, acc0_done, c0_ready = (
            sem(x) for x in ("s16_spread", "p16_ready", "x16_hi", "x16_ready", "acc0_done", "c0_ready"))
        z0_added, z1_added, z_ready = (sem(x) for x in ("z0_added", "z1_added", "z_ready"))
        h1_sum, h1_ready, h2_sum, h2_ready, y_sum, y_ready, stored = (
            sem(x) for x in ("h1_sum", "h1_ready", "h2_sum", "h2_ready", "y_sum", "y_ready", "stored"))

        def two(ap):
            return ap.unsqueeze(1).to_broadcast([P, 2, COLS])

        block = ctx.enter_context(nc.Block())

        @block.sync
        def _(sp):
            sp.dma_start(ids_sb[:], ids.rearrange("(g p) f -> p g f", p=P)).then_inc(ids_in, 16)
            sp.dma_start(raw[:, F * N + 9 * N:F * N + 9 * N + F + 6 * P],
                         consts[:, 0:F + 6 * P]).then_inc(const_in, 16)
            sp.dma_start(ident[:], consts[:, F + 6 * P:]).then_inc(const_in, 16)
            sp.dma_start(w0a_raw, w0a).then_inc(f0_in, 16)
            sp.dma_start(w0b_raw, w0b).then_inc(f0_in, 16)
            sp.dma_start(w1_raw, w1).then_inc(f1_in, 16)
            sp.dma_start(wt1_sb[:], wt1.rearrange("(t p) n -> p t n", p=P)).then_inc(tower_in, 16)
            sp.dma_start(wt1d_sb[:], wt1d).then_inc(tower_in, 16)
            sp.dma_start(wt2_sb[:], wt2.rearrange("(t p) n -> p t n", p=P)).then_inc(tower_in, 16)
            sp.dma_start(wt3_sb[:], wt3).then_inc(tower_in, 16)
            sp.dma_start(bt1_sb[:], bt1).then_inc(tower_in, 16)
            sp.dma_start(bt2_sb[:], bt2).then_inc(tower_in, 16)
            sp.dma_start(dense_sb[:], dense_t).then_inc(tower_in, 16)
            sp.wait_ge(y_ready, 2)
            sp.dma_start(out.unsqueeze(0), y_sb).then_inc(stored, 16)
            sp.wait_ge(stored, 16)

        @block.gpsimd
        def _(pool):
            def load_ids(g):
                nc.gpsimd.tensor_copy(ids_now[:], ids_sb[:, g, :] if isinstance(g, int)
                                      else ids_sb[:, bass.ds(g, 1), :].rearrange("p a f -> p (a f)")
                                      ).then_inc(ids_ready, 1)
                pool.wait_ge(ids_ready, g + 1)

            def gather(f):
                nc.gpsimd.indirect_dma_start(
                    rows[:, f, :], None, tables[f],
                    bass.IndirectOffsetOnAxis(ap=ids_now[:, f:f + 1], axis=0)).then_inc(gathered, 16)

            def split_rows(g, parity, first=False):
                pool.wait_ge(gathered, (g + 1) * (16 * F))
                if not first:
                    pool.wait_ge(staged, (g - 1) * CPG)
                src = rows[:].rearrange("p f d -> p d f")
                if isinstance(parity, int):
                    half = emb[:, CPG * parity:CPG * (parity + 1), :, :]
                else:
                    half = emb[:, bass.ds(parity * CPG, CPG), :, :]
                half = half.rearrange("p c d x -> p (c d) x")
                nc.gpsimd.tensor_copy(half[:, :, 0:F], src).then_inc(emb_hi, 1)
                pool.wait_ge(emb_hi, g + 1)
                nc.gpsimd.tensor_tensor(half[:, :, F:2 * F], src, half[:, :, 0:F].bitcast(F32),
                                        ALU.subtract).then_inc(emb_ready, 1)
                pool.wait_ge(emb_ready, g + 1)

            def sub(s, base=None, per=0):
                def n(rate, const):
                    return const if base is None else base * (rate * per) + const
                pool.wait_ge(hi_ready, n(PER, s + 1))
                if s >= LOS:
                    pool.wait_ge(step_done, n(PER, s + 1 - LOS))
                nc.gpsimd.tensor_tensor(lo[:, s % LOS], prod[:, s % PRODS],
                                        hi[:, s % HIS].bitcast(F32), ALU.subtract).then_inc(lo_pool, 1)

            def iteration(k, fields, base=None, per=0):
                js = range(HALF if k == LAST else PER)
                mine = [s for s in (HEAD + k * PER + j for j in js) if not on_dve(s)]
                for i, s in enumerate(mine):
                    sub(s, base, per)
                    for f in fields[len(fields) * i // len(mine):len(fields) * (i + 1) // len(mine)]:
                        gather(f)

            pool.wait_ge(ids_in, 16)
            load_ids(0)
            for f in range(F):
                gather(f)
            split_rows(0, 0, first=True)
            load_ids(1)
            for s in range(HEAD):
                if not on_dve(s):
                    sub(s)
            for k in range(6):
                iteration(k, range(6 * k, min(6 * k + 6, F)))
            split_rows(1, 1, first=True)
            with pool.Fori(0, GROUPS - 2) as i:
                load_ids(i + 2)
                for m in range(CPG):
                    fields = range(5 * m, min(5 * m + 5, F))
                    iteration(6 + m, fields, i, CPG)
                split_rows(i + 2, i % 2)
            for k in range(6 + CPG * (GROUPS - 2), CHUNKS):
                iteration(k, range(0))

        @block.scalar
        def _(act):
            def stage_chunk(c, ring_at, group):
                act.wait_ge(emb_ready, group + 1)
                if not (isinstance(c, int) and c == 0):
                    act.wait_ge(turned, c)
                src = emb[:].bitcast(F32).rearrange("p a d x -> p (a d x)")
                size = DPC * 2 * F
                src = (src[:, bass.ds(ring_at * size, size)] if not isinstance(ring_at, int)
                       else src[:, ring_at * size:(ring_at + 1) * size])
                src = src.rearrange("p (d x) -> p d x", d=DPC)
                nc.scalar.activation(stage[:], src.unsqueeze(2).to_broadcast([P, DPC, 2, 2 * F]),
                                     ACT.Copy).then_inc(staged, 1)

            def store_est(c, parity):
                act.wait_ge(turned, c + 1)
                nc.scalar.activation(est[:, parity], misc[:], ACT.Copy).then_inc(est_ready, 1)

            def store_e4(c):
                act.wait_ge(e4_spread, c + 1)
                nc.scalar.activation(e4[:], misc[:], ACT.Copy).then_inc(e4_ready, 1)

            def round_16(c):
                act.wait_ge(p16_ready, c + 1)
                if not (isinstance(c, int) and c == 0):
                    act.wait_ge(acc0_done, c)
                nc.scalar.activation(x16[:], p16[:], ACT.Copy).then_inc(x16_hi, 1)

            def relu_c0(c, parity, used=None):
                act.wait_ge(acc0_done, c + 1)
                if used is not None:
                    act.wait_ge(prod_ready, used)
                nc.scalar.activation(c0[:, parity], acc0[:], ACT.Relu).then_inc(c0_ready, 1)

            def round_step(s, n):
                act.wait_ge(prod_ready, n(PER, s + 1))
                if s >= HIS:
                    act.wait_ge(step_done, n(PER, s + 1 - HIS))
                nc.scalar.activation(hi[:, s % HIS], prod[:, s % PRODS], ACT.Copy).then_inc(hi_ready, 1)

            def iteration(k, base=None):
                def n(rate, const):
                    return const if base is None else base * (rate * 2) + const
                for j in range(HALF if k == LAST else PER):
                    s = HEAD + k * PER + j
                    round_step(s, n)
                    j = place(s)
                    if j == 2 and k < LAST:
                        round_16(n(1, k + 1))
                    if j == 5 and k + 2 < CHUNKS:
                        c = n(1, k + 2)
                        stage_chunk(c, c % (2 * CPG), c // CPG)
                    if j == 6 and k < LAST:
                        relu_c0(n(1, k + 1), (k + 1) % 2, n(PER, last_step(k - 1) + 1))
                    if j == 9 and k + 2 < CHUNKS:
                        store_est(n(1, k + 2), k % 2)
                    if j == 12 and k + 2 < CHUNKS:
                        store_e4(n(1, k + 2))

            def static(rate, const):
                return const

            act.wait_ge(const_in, 32)
            nc.scalar.activation(shift[:], shift_raw, ACT.Copy).then_inc(consts_ready, 1)
            nc.scalar.activation(pick[:], pick_raw.unsqueeze(2).to_broadcast([P, F, P]),
                                 ACT.Copy).then_inc(consts_ready, 1)
            act.wait_ge(f0_in, 32)
            nc.scalar.activation(f16[:], w0a_raw[:, 4, :], ACT.Copy).then_inc(split_hi, 1)
            act.wait_ge(f0_sum, 1)
            nc.scalar.activation(f0h[:], w0a_raw[:, 0:4, :], ACT.Copy).then_inc(split_hi, 1)
            act.wait_ge(f1_in, 16)
            nc.scalar.activation(f1h[:], w1_raw, ACT.Copy).then_inc(split_hi, 1)

            stage_chunk(0, 0, 0)
            store_est(0, 0)
            store_e4(0)
            stage_chunk(1, 1, 0)
            round_step(0, static)
            round_step(1, static)
            round_16(0)
            relu_c0(0, 0)
            for s in range(2, HEAD):
                round_step(s, static)
                if s == 3:
                    store_est(1, 1)
                if s == 5:
                    store_e4(1)
            with act.Fori(0, (CHUNKS - 2) // 2) as i:
                iteration(0, i)
                iteration(1, i)
            iteration(LAST - 1)
            iteration(LAST)

            act.wait_ge(tower_in, 16 * 7)
            for half in range(2):
                for m in range(H1 // P):
                    act.wait_ge(h1_sum, 4 * half + m + 1)
                    if half:
                        act.wait_ge(h2_sum, 2)
                    nc.scalar.activation(h1[:, m], spread[:, m // 2, m % 2], ACT.Relu,
                                         bias=bt1_sb[:, m:m + 1]).then_inc(h1_ready, 1)
                for m in range(H2 // P):
                    act.wait_ge(h2_sum, 2 * half + m + 1)
                    if half:
                        act.wait_ge(y_sum, 1)
                    nc.scalar.activation(h2[:, m], acc1[:, m], ACT.Relu,
                                         bias=bt2_sb[:, m:m + 1]).then_inc(h2_ready, 1)
                act.wait_ge(y_sum, half + 1)
                nc.scalar.activation(y_sb[:, 512 * half:512 * (half + 1)], acc0[0:1, :],
                                     ACT.Copy).then_inc(y_ready, 1)

        @block.vector
        def _(dve):
            def product(s, n):
                layer, c, item = decode(s)
                dve.wait_ge(spread_ready, n(PER, s + 1))
                if s >= PRODS:
                    old = s - PRODS
                    if on_dve(old):
                        dve.wait_ge(lo_dve, n(DVE_PER, dve_before(old) + 1))
                    else:
                        dve.wait_ge(lo_pool, n(POOL_PER, pool_before(old) + 1))
                if layer == 0:
                    if item == 0:
                        dve.wait_ge(e4_ready, n(1, c + 1))
                    other = e4[:]
                else:
                    if item == 0:
                        dve.wait_ge(c0_ready, n(1, c + 1))
                    other = c0[:, c % 2]
                nc.vector.tensor_tensor(prod[:, s % PRODS], spread[:, s % SPREADS], two(other),
                                        ALU.mult).then_inc(prod_ready, 1)

            def sub(s, n):
                dve.wait_ge(hi_ready, n(PER, s + 1))
                if s >= LOS:
                    dve.wait_ge(step_done, n(PER, s + 1 - LOS))
                nc.vector.tensor_tensor(lo[:, s % LOS], prod[:, s % PRODS],
                                        hi[:, s % HIS].bitcast(F32), ALU.subtract).then_inc(lo_dve, 1)

            def product_16(c):
                dve.wait_ge(s16_spread, c + 1)
                if not (isinstance(c, int) and c == 0):
                    dve.wait_ge(x16_ready, c)
                nc.vector.tensor_tensor(p16[:], misc[:], e4[:], ALU.mult).then_inc(p16_ready, 1)

            def lo_16(c):
                dve.wait_ge(x16_hi, c + 1)
                nc.vector.tensor_tensor(x16[F:2 * F], p16[F:2 * F], x16[F:2 * F].bitcast(F32),
                                        ALU.subtract).then_inc(x16_ready, 1)

            def zslice(layer, g):
                if isinstance(g, int):
                    return zacc[:, layer, g, :]
                return zacc[:, layer, bass.ds(g, 1), :].rearrange("p a c -> p (a c)")

            def add_z0(c, parity, g):
                dve.wait_ge(z0_added, c + 1)
                z = zslice(0, g)
                nc.vector.tensor_tensor(z, c0[:, parity], z, ALU.add).then_inc(z0_added, 1)

            def add_z1(c, parity, g, done):
                dve.wait_ge(step_done, done)
                dve.wait_ge(z1_added, c + 1)
                z = zslice(1, g)
                nc.vector.scalar_tensor_tensor(out=z, in0=acc1[:, parity], scalar=0.0, in1=z,
                                               op0=ALU.max, op1=ALU.add).then_inc(z1_added, 1)

            def iteration(k, base=None):
                def n(rate, const):
                    return const if base is None else base * (rate * 2) + const
                c = n(1, k)
                for j in range(HALF if k == LAST else PER):
                    s = HEAD + k * PER + j
                    product(s, n)
                    if on_dve(s - DELTA):
                        sub(s - DELTA, n)
                    j = place(s)
                    if j == 2 and k < LAST:
                        product_16(n(1, k + 1))
                    if j == 4 and k < LAST:
                        lo_16(n(1, k + 1))
                    if j == 7:
                        add_z0(c, k % 2, c // CPG)
                    if j == 15:
                        add_z1(c, k % 2, c // CPG, n(PER, last_step(k) + 1))

            def static(rate, const):
                return const

            dve.wait_ge(f0_in, 32)
            nc.vector.tensor_tensor(w0a_raw[:, 0:4, :], w0a_raw[:, 0:4, :], w0b_raw,
                                    ALU.add).then_inc(f0_sum, 1)
            dve.wait_ge(split_hi, 1)
            nc.vector.tensor_tensor(f16[2 * F:3 * F], w0a_raw[2 * F:3 * F, 4, :],
                                    f16[2 * F:3 * F].bitcast(F32), ALU.subtract).then_inc(split_lo, 1)
            nc.vector.memset(f16[3 * F:4 * F].bitcast(F32), 0.0).then_inc(split_lo, 1)
            dve.wait_ge(split_hi, 2)
            nc.vector.tensor_tensor(f0l[:], w0a_raw[:, 0:4, :], f0h[:].bitcast(F32),
                                    ALU.subtract).then_inc(split_lo, 1)
            dve.wait_ge(split_hi, 3)
            nc.vector.tensor_tensor(f1l[:], w1_raw, f1h[:].bitcast(F32),
                                    ALU.subtract).then_inc(split_lo, 1)
            dve.wait_ge(consts_ready, 2)
            dve.wait_ge(split_lo, 4)
            nc.vector.memset(zacc[:, 0], 0.0).then_inc(z0_added, 1)
            nc.vector.memset(zacc[:, 1], 0.0).then_inc(z1_added, 1)

            product(0, static)
            product(1, static)
            product_16(0)
            if on_dve(0):
                sub(0, static)
            if on_dve(1):
                sub(1, static)
            lo_16(0)
            for s in range(2, HEAD):
                product(s, static)
                if s - DELTA >= 2 and on_dve(s - DELTA):
                    sub(s - DELTA, static)
            with dve.Fori(0, (CHUNKS - 2) // 2) as i:
                iteration(0, i)
                iteration(1, i)
            iteration(LAST - 1)
            iteration(LAST)
            for s in range(STEPS - DELTA, STEPS):
                if on_dve(s):
                    sub(s, static)
            add_z1(LAST, LAST % 2, GROUPS - 1, STEPS)

            dve.wait_ge(z0_added, CHUNKS + 1)
            dve.wait_ge(z1_added, CHUNKS + 1)
            for half in range(2):
                for layer in range(2):
                    gs = slice(half * GROUPS // 2, (half + 1) * GROUPS // 2)
                    nc.vector.tensor_reduce(
                        zsum[:, layer, 512 * half:512 * (half + 1)].rearrange("p (g b) -> p g b", b=P),
                        zacc[:, layer, gs, :].rearrange("p g (d b) -> p g b d", b=P),
                        AX.X, ALU.add).then_inc(z_ready, 1)

        @block.tensor
        def _(pe):
            def spread_step(s, n):
                layer, c, item = decode(s)
                if s >= SPREADS:
                    pe.wait_ge(prod_ready, n(PER, s + 1 - SPREADS))
                if layer == 0 and item == 0:
                    pe.wait_ge(est_ready, n(1, c + 1))
                for i in range(2):
                    lhs = shift[:, 2 * item + i] if layer == 0 else pick[:, 2 * item + i]
                    mm = pe.matmul(spread[:, s % SPREADS, i], lhs, est[:, c % 2], start=True, stop=True)
                mm.then_inc(spread_ready, 1)
                if layer == 0 and item == 1:
                    pe.wait_ge(e4_ready, n(1, c + 1))
                    pe.matmul(misc[:], shift[:, 4], est[:, c % 2], start=True,
                              stop=True).then_inc(s16_spread, 1)

            def products(s, n):
                layer, c, item = decode(s)
                if on_dve(s):
                    pe.wait_ge(lo_dve, n(DVE_PER, dve_before(s) + 1))
                else:
                    pe.wait_ge(lo_pool, n(POOL_PER, pool_before(s) + 1))
                if layer == 0 and item == 0 and not (s < HEAD):
                    pe.wait_ge(c0_ready, n(1, c))
                if layer == 1 and item == 0 and not (s < HEAD):
                    pe.wait_ge(z1_added, n(1, c))
                wh, wl = (f0h, f0l) if layer == 0 else (f1h, f1l)
                acc = acc0[:] if layer == 0 else acc1[:, c % 2]
                for i in range(2):
                    w = 2 * item + i
                    h, l = hi[:, s % HIS, i], lo[:, s % LOS, i]
                    pe.matmul(acc, wl[:, w], h, start=(w == 0), stop=False)
                    pe.matmul(acc, wh[:, w], l, start=False, stop=False)
                    mm = pe.matmul(acc, wh[:, w], h, start=False,
                                   stop=(layer == 1 and w == F - 1))
                mm.then_inc(step_done, 1)

            def products_16(c):
                pe.wait_ge(x16_ready, c + 1)
                pe.matmul(acc0[:], f16[:], x16[:], start=False, stop=True).then_inc(acc0_done, 1)

            def turn(c):
                pe.wait_ge(staged, c + 1)
                if not (isinstance(c, int) and c == 0):
                    pe.wait_ge(p16_ready, c)
                for d in range(DPC):
                    src = stage[:, d].rearrange("p r x -> p (r x)")
                    t = pe.transpose(misc[:, d * P:(d + 1) * P], src, ident[:])
                t.then_inc(turned, 1)

            def spread_e4(c, parity):
                pe.wait_ge(est_ready, c + 1)
                pe.matmul(misc[:], shift[:, 5], est[:, parity], start=True,
                          stop=True).then_inc(e4_spread, 1)

            def iteration(k, base=None):
                def n(rate, const):
                    return const if base is None else base * (rate * 2) + const
                for j in range(HALF if k == LAST else PER):
                    s = HEAD + k * PER + j
                    if s + AHEAD < STEPS:
                        spread_step(s + AHEAD, n)
                    products(s, n)
                    j = place(s)
                    if j == 2 and k < LAST:
                        products_16(n(1, k + 1))
                    if j == 5 and k + 2 < CHUNKS:
                        turn(n(1, k + 2))
                    if j == 8 and k + 2 < CHUNKS:
                        spread_e4(n(1, k + 2), k % 2)

            def static(rate, const):
                return const

            pe.wait_ge(const_in, 32)
            pe.wait_ge(consts_ready, 2)
            turn(0)
            spread_e4(0, 0)
            spread_step(0, static)
            spread_step(1, static)
            pe.wait_ge(split_hi, 3)
            pe.wait_ge(split_lo, 4)
            products(0, static)
            products(1, static)
            products_16(0)
            for s in range(2, 2 + AHEAD):
                spread_step(s, static)
            for s in range(2, HEAD):
                if s == 3:
                    turn(1)
                if s == 5:
                    spread_e4(1, 1)
                spread_step(s + AHEAD, static)
                products(s, static)
            with pe.Fori(0, (CHUNKS - 2) // 2) as i:
                iteration(0, i)
                iteration(1, i)
            iteration(LAST - 1)
            iteration(LAST)

            pe.wait_ge(tower_in, 16 * 7)
            for half in range(2):
                cols = slice(512 * half, 512 * (half + 1))
                pe.wait_ge(z_ready, 2 * half + 2)
                for m in range(H1 // P):
                    ms = slice(m * P, (m + 1) * P)
                    if half:
                        pe.wait_ge(h1_ready, m + 1)
                    o = spread[:, m // 2, m % 2]
                    pe.matmul(o, wt1_sb[:, 0, ms], zsum[:, 0, cols], start=True, stop=False)
                    pe.matmul(o, wt1_sb[:, 1, ms], zsum[:, 1, cols], start=False, stop=False)
                    pe.matmul(o, wt1d_sb[:, ms], dense_sb[:, cols], start=False,
                              stop=True).then_inc(h1_sum, 1)
                for m in range(H2 // P):
                    if half:
                        pe.wait_ge(h2_ready, m + 1)
                    for t in range(H1 // P):
                        if m == 0:
                            pe.wait_ge(h1_ready, 4 * half + t + 1)
                        mm = pe.matmul(acc1[:, m], wt2_sb[:, t, m * P:(m + 1) * P], h1[:, t],
                                       start=(t == 0), stop=(t == H1 // P - 1))
                    mm.then_inc(h2_sum, 1)
                if half:
                    pe.wait_ge(y_ready, 1)
                for t in range(H2 // P):
                    pe.wait_ge(h2_ready, 2 * half + t + 1)
                    mm = pe.matmul(acc0[0:1, :], wt3_sb[:, t:t + 1], h2[:, t],
                                   start=(t == 0), stop=(t == H2 // P - 1))
                mm.then_inc(y_sum, 1)


def layout_constants():
    k = np.arange(P)
    out = np.zeros((P, F + 7 * P), np.float32)
    half = k < 2 * F
    out[:, :F] = (k[:, None] % F == np.arange(F)[None, :]) & half[:, None]
    col = np.arange(P)
    for t in range(6):
        s = 4 * t + col // F if t < 4 else np.full(P, 16 if t == 4 else 0)
        src = (col % F + s) % F
        out[:, F + t * P:F + (t + 1) * P] = (k[:, None] % F == src[None, :]) & half[:, None]
    out[:, F + 6 * P:] = np.eye(P)
    return out


def kernel(**inputs):
    import concourse.bacc as bacc
    from concourse.bass_utils import run_bass_kernel_spmd

    x = {k: np.asarray(v) for k, v in inputs.items()}
    f0 = x["L0_rec_filter_0"][0].reshape(F, F, N)
    f = np.arange(F)
    w0a = np.zeros((P, 5, N), np.float32)
    w0b = np.zeros((P, 4, N), np.float32)
    for s in range(16):
        r = slice((s % 4) * F, (s % 4 + 1) * F)
        w0a[r, s // 4] = f0[f, (f + s) % F]
        if s:
            w0b[r, s // 4] = f0[(f + s) % F, f]
    for r in range(4):
        w0a[r * F:(r + 1) * F, 4] = f0[f, (f + 16) % F]
    w1 = np.ascontiguousarray(x["L0_rec_filter_1"][0].reshape(F, N, N).transpose(1, 0, 2))
    arrays = {f"tbl_{i}": x[f"tbl_{i}"] for i in range(F)}
    arrays |= {
        "ids": x["ids"], "w0a": w0a, "w0b": w0b, "w1": w1, "consts": layout_constants(),
        "dense_t": np.ascontiguousarray(x["dense_ctx"].T),
        "wt1": x["W_top1"][:2 * N], "wt1d": x["W_top1"][2 * N:], "wt2": x["W_top2"],
        "wt3": np.ascontiguousarray(x["W_top3"].reshape(H2 // P, P).T),
        "bt1": np.ascontiguousarray(x["b_top1"].reshape(H1 // P, P).T),
        "bt2": np.ascontiguousarray(x["b_top2"].reshape(H2 // P, P).T),
    }
    arrays = {f"in_{k}": np.ascontiguousarray(v) for k, v in arrays.items()}
    nc = bacc.Bacc("TRN2", target_bir_lowering=False, num_devices=1)
    ap = {k: nc.dram_tensor(k, v.shape, mybir.dt.from_np(v.dtype), kind="ExternalInput").ap()
          for k, v in arrays.items()}
    out = nc.dram_tensor("out", (B,), F32, kind="ExternalOutput").ap()
    build(nc, [ap[f"in_tbl_{i}"] for i in range(F)], ap["in_ids"], ap["in_w0a"], ap["in_w0b"],
          ap["in_w1"], ap["in_consts"], ap["in_dense_t"], ap["in_wt1"], ap["in_wt1d"], ap["in_wt2"],
          ap["in_wt3"], ap["in_bt1"], ap["in_bt2"], out)
    r = run_bass_kernel_spmd(nc, [arrays], core_ids=[0])
    return r.results[0]["out"].reshape(B, 1)
```

```python
from contextlib import ExitStack

import numpy as np

import concourse.bass as bass
from concourse import mybir

ALU = mybir.AluOpType
ACT = mybir.ActivationFunctionType
AX = mybir.AxisListType
F32 = mybir.dt.float32
F32R = mybir.dt.float32r
I32 = mybir.dt.int32

P = 128
B, F, D, N = 1024, 32, 32, 128
GROUPS = B // P
CPG = 8
DPC = D // CPG
COLS = DPC * P
CHUNKS = GROUPS * CPG
LAST = CHUNKS - 1
TILES0 = 4
DENSE, H1, H2 = 16, 512, 256

HPT, MPT = 4, 32
HG, MG = F // HPT, N // MPT
PAIRS = HG * MG // 2
EARLY, LATE = 2, 14
PER = 2 + PAIRS
POS0 = (0, 5)
POS1 = [j for j in range(PER) if j not in POS0]
HEAD = 2 + EARLY
STEPS = CHUNKS * PER

AHEAD = 6
PE_16, PE_TURN, PE_E4 = 5, 9, 11
ACT_16, ACT_C0, ACT_STAGE, ACT_EST, ACT_E4 = 6, 8, 8, 13, 15
DVE_16, DVE_LO16, DVE_Z0, DVE_STAGE, DVE_Z1 = 5, 7, 12, 11, 2
DELTA = 2
BANKS, PRODS, HIS, LOS = 4, 9, 7, 4
POOL, DVE, FULL = range(3)
KIND = [{"P": POOL, "D": DVE, "F": FULL}[x] for x in "PPDFPPDPFPPDFPPDFP"]


def place(s):
    if s < 2:
        return POS0[s]
    if s < HEAD:
        return s + PER - HEAD
    k, j = divmod(s - HEAD, PER)
    return POS1[j] if k == LAST else j


def decode(s):
    j = place(s)
    k = -1 if s < HEAD else (s - HEAD) // PER
    if j in POS0:
        return 0, k + 1, POS0.index(j)
    i = POS1.index(j)
    return (1, k, i + EARLY) if i < LATE else (1, k + 1, i - LATE)


def kind(s):
    return KIND[place(s)]


BEFORE = [[0, 0, 0]]
for _s in range(STEPS):
    BEFORE.append([c + (kind(_s) == x) for x, c in enumerate(BEFORE[-1])])
RATE = [KIND.count(x) for x in range(3)]
SPLIT_RATE = RATE[POOL] + RATE[DVE]


def before(s, x):
    return BEFORE[s][x]


def split_before(s):
    return BEFORE[s][POOL] + BEFORE[s][DVE]


def split_step(i):
    s = i
    while split_before(s + 1) <= i:
        s += 1
    return s


BANK, FREED = [], []
_last, _n = {}, 0
for _s in range(STEPS):
    _layer, _, _item = decode(_s)
    _w = 2 if _layer == 0 else 1
    if _layer == 1 and _item % 2:
        BANK.append(BANK[-1])
        FREED.append(None)
    else:
        _n += _n % _w
        BANK.append(_n % BANKS)
        FREED.append(max((_last.get((_n + x) % BANKS, -1) for x in range(_w))))
        _n += _w
    for _x in range(_w):
        _last[BANK[-1] + _x] = _s


def last_step(chunk):
    return HEAD + PER * chunk + (1 if chunk < LAST else -1) + LATE


ITEM_KIND = {decode(HEAD + j)[2]: KIND[j] for j in POS1}
SPLIT_ITEMS = [i for i in range(PAIRS) if ITEM_KIND[i] != FULL]
FULL_ITEMS = [i for i in range(PAIRS) if ITEM_KIND[i] == FULL]
NSPLIT = 2 * len(SPLIT_ITEMS)


def build(nc, tables, ids, w0a, w0b, w1, consts, dense_t, wt1, wt1d, wt2, wt3, bt1, bt2, out):
    with ExitStack() as ctx:
        def sb(name, shape, dt=F32):
            return ctx.enter_context(nc.sbuf_tensor(name, shape, dt))

        def sem(name):
            return ctx.enter_context(nc.semaphore(name))

        espread = ctx.enter_context(nc.psum_tensor("espread", [P, BANKS, COLS], F32))
        acc1 = ctx.enter_context(nc.psum_tensor("acc1", [P, 2, COLS], F32))
        acc0 = ctx.enter_context(nc.psum_tensor("acc0", [P, COLS], F32))
        misc = ctx.enter_context(nc.psum_tensor("misc", [P, COLS], F32))

        prod = sb("prod", [P, PRODS, 2, COLS])
        hi = sb("hi", [P, HIS, 2, COLS], F32R)
        lo = sb("lo", [P, LOS, 2, COLS], F32R)

        f1h = sb("f1h", [P, NSPLIT, N], F32R)
        f1l = sb("f1l", [P, NSPLIT, N], F32R)
        f1 = sb("f1", [P, HG * MG - NSPLIT, N])
        f0h = sb("f0h", [P, TILES0, N], F32R)
        f0l = sb("f0l", [P, TILES0, N], F32R)
        f16 = sb("f16", [P, N], F32R)
        pick = sb("pick", [P, HG, P], F32R)
        shift = sb("shift", [P, 6, P], F32R)
        ident = sb("ident", [P, P])

        ids_sb = sb("ids_sb", [P, GROUPS, F], I32)
        ids_now = sb("ids_now", [P, F], I32)
        rows = sb("rows", [P, F, D])
        emb = sb("emb", [P, 2, F, D])
        stage = sb("stage", [P, DPC, 4, F], F32R)
        est = sb("est", [P, 2, COLS], F32R)
        e4 = sb("e4", [P, COLS])
        cspread = sb("cspread", [P, 2, MG, COLS])
        p16 = sb("p16", [P, COLS])
        x16 = sb("x16", [P, COLS], F32R)

        zacc = sb("zacc", [P, 2, GROUPS, COLS])
        wt3_sb = sb("wt3_sb", [P, H2 // P])
        bt1_sb = sb("bt1_sb", [P, H1 // P])
        bt2_sb = sb("bt2_sb", [P, H2 // P])

        raw = zacc[:].rearrange("p a g c -> p (a g c)")
        w1_raw = raw[:, 0:NSPLIT * N].rearrange("p (t n) -> p t n", n=N)
        at = NSPLIT * N
        w0a_raw = raw[:, at:at + 5 * N].rearrange("p (t n) -> p t n", n=N)
        at += 5 * N
        w0b_raw = raw[:, at:at + 4 * N].rearrange("p (t n) -> p t n", n=N)
        at += 4 * N
        const_raw = raw[:, at:at + (HG + 6) * P]
        pick_raw = const_raw[:, 0:HG * P].rearrange("p (t n) -> p t n", n=P)
        shift_raw = const_raw[:, HG * P:].rearrange("p (t n) -> p t n", n=P)
        old = cspread[:, LAST % 2].rearrange("p g c -> p (g c)")
        zsum = old.rearrange("p (l b) -> p l b", l=2)
        old = cspread[:, 1 - LAST % 2].rearrange("p g c -> p (g c)")
        wt1_sb = old[:, 0:2 * H1].rearrange("p (t n) -> p t n", n=H1)
        wt2_sb = old[:, 2 * H1:].rearrange("p (t n) -> p t n", n=H2)
        old = emb[:].rearrange("p a f d -> p (a f d)")
        dense_sb, wt1d_sb = old[0:DENSE, 0:B], old[0:DENSE, B:B + H1]
        ring = prod[:].rearrange("p a b c -> p (a b c)")
        h1 = ring[:, 0:4 * 512].rearrange("p (m c) -> p m c", c=512)
        h2 = ring[:, 4 * 512:6 * 512].rearrange("p (m c) -> p m c", c=512)
        y_sb = ring[0:1, 6 * 512:8 * 512]

        f1_full_in = sem("f1_full_in")
        ids_in, f1_in, f0_in, const_in, tower_in = (
            sem(x) for x in ("ids_in", "f1_in", "f0_in", "const_in", "tower_in"))
        split_hi, f0_sum, split_lo, consts_ready, cleared = (
            sem(x) for x in ("split_hi", "f0_sum", "split_lo", "consts_ready", "cleared"))
        ids_ready, gathered, emb_ready = (sem(x) for x in ("ids_ready", "gathered", "emb_ready"))
        stage_zero, stage_hi, staged, turned, est_ready, e4_spread, e4_ready = (
            sem(x) for x in ("stage_zero", "stage_hi", "staged", "turned", "est_ready", "e4_spread", "e4_ready"))
        spread_ready, prod_ready, hi_ready, lo_pool, lo_dve, step_done = (
            sem(x) for x in ("spread_ready", "prod_ready", "hi_ready", "lo_pool", "lo_dve", "step_done"))
        s16_spread, p16_ready, x16_hi, x16_ready, acc0_done, c0_ready = (
            sem(x) for x in ("s16_spread", "p16_ready", "x16_hi", "x16_ready", "acc0_done", "c0_ready"))
        cspread_in = [[sem("cspread_even_1"), sem("cspread_even_23")],
                      [sem("cspread_odd_1"), sem("cspread_odd_23")]]
        z0_added, z1_added, z_ready = (sem(x) for x in ("z0_added", "z1_added", "z_ready"))
        h1_sum, h1_ready, h2_sum, h2_ready, y_sum, y_ready, stored = (
            sem(x) for x in ("h1_sum", "h1_ready", "h2_sum", "h2_ready", "y_sum", "y_ready", "stored"))

        CSPREAD = [16 * HPT, 16 * HPT * 2]
        TOWER_IN = 16 * 7

        def two(ap):
            return ap.unsqueeze(1).to_broadcast([P, 2, COLS])

        def emb_chunk(c):
            g = c // CPG
            if isinstance(c, int):
                return emb[:, g % 2, :, c % CPG * DPC:(c % CPG + 1) * DPC].rearrange("p f d -> p d f")
            return emb[:, bass.ds(g % 2, 1), :, bass.ds((c % CPG) * DPC, DPC)].rearrange(
                "p a f d -> p d (a f)")

        block = ctx.enter_context(nc.Block())

        @block.sync
        def _(sp):
            sp.dma_start(ids_sb[:], ids.rearrange("(g p) f -> p g f", p=P)).then_inc(ids_in, 16)
            sp.dma_start(const_raw, consts[:, 0:(HG + 6) * P]).then_inc(const_in, 16)
            sp.dma_start(ident[:], consts[:, (HG + 6) * P:]).then_inc(const_in, 16)
            sp.dma_start(w0a_raw, w0a).then_inc(f0_in, 16)
            sp.dma_start(w0b_raw, w0b).then_inc(f0_in, 16)
            sp.dma_start(w1_raw, w1[:, 0:NSPLIT]).then_inc(f1_in, 16)
            sp.dma_start(f1[:], w1[:, NSPLIT:]).then_inc(f1_full_in, 16)
            sp.dma_start(wt3_sb[:], wt3).then_inc(tower_in, 16)
            sp.dma_start(bt1_sb[:], bt1).then_inc(tower_in, 16)
            sp.dma_start(bt2_sb[:], bt2).then_inc(tower_in, 16)

            def spread_c0(c, parity):
                sp.wait_ge(c0_ready, c + 1)
                for q in range(1, MG):
                    for h in range(HPT):
                        m = MPT * ((q + h) % MG)
                        sp.dma_start(cspread[MPT * h:MPT * (h + 1), parity, q, :],
                                     cspread[m:m + MPT, parity, 0, :]
                                     ).then_inc(cspread_in[parity][q // 2], 16)

            spread_c0(0, 0)
            spread_c0(1, 1)
            with sp.Fori(0, (CHUNKS - 2) // 2) as i:
                for c in (2, 3):
                    spread_c0(i * 2 + c, c % 2)
            sp.wait_ge(staged, CHUNKS)
            sp.dma_start(wt1d_sb, wt1d).then_inc(tower_in, 16)
            sp.dma_start(dense_sb, dense_t).then_inc(tower_in, 16)
            sp.wait_ge(prod_ready, last_step(LAST - 1) + 1)
            sp.dma_start(wt1_sb, wt1.rearrange("(t p) n -> p t n", p=P)).then_inc(tower_in, 16)
            sp.dma_start(wt2_sb, wt2.rearrange("(t p) n -> p t n", p=P)).then_inc(tower_in, 16)
            sp.wait_ge(y_ready, 2)
            sp.dma_start(out.unsqueeze(0), y_sb).then_inc(stored, 16)
            sp.wait_ge(stored, 16)

        @block.gpsimd
        def _(pool):
            def load_ids(g):
                nc.gpsimd.tensor_copy(ids_now[:], ids_sb[:, g, :] if isinstance(g, int)
                                      else ids_sb[:, bass.ds(g, 1), :].rearrange("p a f -> p (a f)")
                                      ).then_inc(ids_ready, 1)
                pool.wait_ge(ids_ready, g + 1)

            def gather(f):
                nc.gpsimd.indirect_dma_start(
                    rows[:, f, :], None, tables[f],
                    bass.IndirectOffsetOnAxis(ap=ids_now[:, f:f + 1], axis=0)).then_inc(gathered, 16)

            def keep_rows(g, parity):
                pool.wait_ge(gathered, (g + 1) * (16 * F))
                if not (isinstance(g, int) and g < 2):
                    pool.wait_ge(staged, (g - 1) * CPG)
                half = emb[:, parity] if isinstance(parity, int) else \
                    emb[:, bass.ds(parity, 1)].rearrange("p a f d -> p (a f) d")
                nc.gpsimd.dma_start(half, rows[:]).then_inc(emb_ready, 16)

            def sub(s, base=None, per=0):
                def n(rate, const):
                    return const if base is None else base * (rate * per) + const
                i = split_before(s)
                pool.wait_ge(hi_ready, n(SPLIT_RATE, i + 1))
                if i >= LOS:
                    pool.wait_ge(step_done, n(PER, split_step(i - LOS) + 1))
                nc.gpsimd.tensor_tensor(lo[:, i % LOS], prod[:, s % PRODS],
                                        hi[:, i % HIS].bitcast(F32), ALU.subtract).then_inc(lo_pool, 1)

            def iteration(k, fields, base=None, per=0):
                js = range(LATE if k == LAST else PER)
                mine = [s for s in (HEAD + k * PER + j for j in js) if kind(s) == POOL]
                for i, s in enumerate(mine):
                    sub(s, base, per)
                    for f in fields[len(fields) * i // len(mine):len(fields) * (i + 1) // len(mine)]:
                        gather(f)

            pool.wait_ge(ids_in, 16)
            load_ids(0)
            for f in range(F):
                gather(f)
            keep_rows(0, 0)
            pool.wait_ge(emb_ready, 16)
            load_ids(1)
            for s in range(HEAD):
                if kind(s) == POOL:
                    sub(s)
            for k in range(5):
                iteration(k, range(F * k // 5, F * (k + 1) // 5))
            keep_rows(1, 1)
            iteration(5, range(0))
            with pool.Fori(0, GROUPS - 2) as i:
                pool.wait_ge(emb_ready, i * 16 + 32)
                load_ids(i + 2)
                for m in range(CPG):
                    iteration(6 + m, range(F * m // 7, F * (m + 1) // 7) if m < 7 else range(0), i, CPG)
                    if m == 6:
                        keep_rows(i + 2, i % 2)
            for k in range(6 + CPG * (GROUPS - 2), CHUNKS):
                iteration(k, range(0))

        @block.scalar
        def _(act):
            def stage_chunk(c):
                static = isinstance(c, int)
                act.wait_ge(emb_ready, (c // CPG + 1) * 16)
                if not (static and c == 0):
                    act.wait_ge(turned, c)
                nc.scalar.activation(stage[:, :, 0, :], emb_chunk(c), ACT.Copy).then_inc(stage_hi, 1)

            def store_est(c, parity):
                act.wait_ge(turned, c + 1)
                nc.scalar.activation(est[:, parity], misc[:], ACT.Copy).then_inc(est_ready, 1)

            def store_e4(c):
                act.wait_ge(e4_spread, c + 1)
                nc.scalar.activation(e4[:], misc[:], ACT.Copy).then_inc(e4_ready, 1)

            def round_16(c):
                act.wait_ge(p16_ready, c + 1)
                if not (isinstance(c, int) and c == 0):
                    act.wait_ge(acc0_done, c)
                nc.scalar.activation(x16[:], p16[:], ACT.Copy).then_inc(x16_hi, 1)

            def relu_c0(c, parity, used=None):
                act.wait_ge(acc0_done, c + 1)
                if not (isinstance(c, int) and c < 2):
                    act.wait_ge(z0_added, c)
                    act.wait_ge(prod_ready, used)
                nc.scalar.activation(cspread[:, parity, 0, :], acc0[:], ACT.Relu).then_inc(c0_ready, 1)

            def round_step(s, n):
                if kind(s) == FULL:
                    return
                i = split_before(s)
                act.wait_ge(prod_ready, n(PER, s + 1))
                if i >= HIS:
                    act.wait_ge(step_done, n(PER, split_step(i - HIS) + 1))
                nc.scalar.activation(hi[:, i % HIS], prod[:, s % PRODS], ACT.Copy).then_inc(hi_ready, 1)

            def iteration(k, base=None):
                def n(rate, const):
                    return const if base is None else base * (rate * 2) + const
                for j in range(LATE if k == LAST else PER):
                    s = HEAD + k * PER + j
                    round_step(s, n)
                    j = place(s)
                    if j == ACT_16 and k < LAST:
                        round_16(n(1, k + 1))
                    if j == ACT_STAGE and k + 2 < CHUNKS:
                        stage_chunk(n(1, k + 2))
                    if j == ACT_C0 and k < LAST:
                        relu_c0(n(1, k + 1), (k + 1) % 2, n(PER, last_step(k - 1) + 1))
                    if j == ACT_EST and k + 2 < CHUNKS:
                        store_est(n(1, k + 2), k % 2)
                    if j == ACT_E4 and k + 2 < CHUNKS:
                        store_e4(n(1, k + 2))

            def static(rate, const):
                return const

            act.wait_ge(const_in, 32)
            nc.scalar.activation(shift[:], shift_raw, ACT.Copy).then_inc(consts_ready, 1)
            nc.scalar.activation(pick[:], pick_raw, ACT.Copy).then_inc(consts_ready, 1)
            act.wait_ge(f0_in, 32)
            nc.scalar.activation(f16[:], w0a_raw[:, 4, :], ACT.Copy).then_inc(split_hi, 1)
            act.wait_ge(f0_sum, 1)
            nc.scalar.activation(f0h[:], w0a_raw[:, 0:4, :], ACT.Copy).then_inc(split_hi, 1)
            act.wait_ge(f1_in, 16)
            nc.scalar.activation(f1h[:], w1_raw, ACT.Copy).then_inc(split_hi, 1)

            stage_chunk(0)
            store_est(0, 0)
            store_e4(0)
            stage_chunk(1)
            round_step(0, static)
            round_step(1, static)
            round_16(0)
            relu_c0(0, 0)
            store_est(1, 1)
            for s in range(2, HEAD):
                round_step(s, static)
                if s == 2:
                    store_e4(1)
            with act.Fori(0, (CHUNKS - 2) // 2) as i:
                iteration(0, i)
                iteration(1, i)
            iteration(LAST - 1)
            iteration(LAST)

            act.wait_ge(tower_in, TOWER_IN)
            for half in range(2):
                for m in range(H1 // P):
                    act.wait_ge(h1_sum, 4 * half + m + 1)
                    if half:
                        act.wait_ge(h2_sum, 2)
                    nc.scalar.activation(h1[:, m], espread[:, m], ACT.Relu,
                                         bias=bt1_sb[:, m:m + 1]).then_inc(h1_ready, 1)
                for m in range(H2 // P):
                    act.wait_ge(h2_sum, 2 * half + m + 1)
                    if half:
                        act.wait_ge(y_sum, 1)
                    nc.scalar.activation(h2[:, m], acc1[:, m], ACT.Relu,
                                         bias=bt2_sb[:, m:m + 1]).then_inc(h2_ready, 1)
                act.wait_ge(y_sum, half + 1)
                nc.scalar.activation(y_sb[:, 512 * half:512 * (half + 1)], acc0[0:1, :],
                                     ACT.Copy).then_inc(y_ready, 1)

        @block.vector
        def _(dve):
            def product(s, n):
                layer, c, item = decode(s)
                dve.wait_ge(spread_ready, n(PER, s + 1))
                if s >= PRODS:
                    old = s - PRODS
                    used, rate = {POOL: (lo_pool, RATE[POOL]), DVE: (lo_dve, RATE[DVE]),
                                  FULL: (step_done, PER)}[kind(old)]
                    count = old if kind(old) == FULL else before(old, kind(old))
                    dve.wait_ge(used, n(rate, count + 1))
                if layer == 0:
                    if item == 0:
                        dve.wait_ge(e4_ready, n(1, c + 1))
                    a, b = espread[:, BANK[s]:BANK[s] + 2], two(e4[:])
                else:
                    if item < 2:
                        dve.wait_ge(cspread_in[c % 2][item], n(CSPREAD[item] // 2, CSPREAD[item] * (c // 2 + 1)))
                    q = 2 * (item % 2)
                    a, b = two(espread[:, BANK[s]]), cspread[:, c % 2, q:q + 2]
                nc.vector.tensor_tensor(prod[:, s % PRODS], a, b, ALU.mult).then_inc(prod_ready, 1)

            def sub(s, n):
                if kind(s) != DVE:
                    return
                i = split_before(s)
                dve.wait_ge(hi_ready, n(SPLIT_RATE, i + 1))
                if i >= LOS:
                    dve.wait_ge(step_done, n(PER, split_step(i - LOS) + 1))
                nc.vector.tensor_tensor(lo[:, i % LOS], prod[:, s % PRODS],
                                        hi[:, i % HIS].bitcast(F32), ALU.subtract).then_inc(lo_dve, 1)

            def stage_lo(c):
                dve.wait_ge(stage_hi, c + 1)
                nc.vector.tensor_tensor(stage[:, :, 1, :], emb_chunk(c), stage[:, :, 0, :].bitcast(F32),
                                        ALU.subtract).then_inc(staged, 1)

            def product_16(c):
                dve.wait_ge(s16_spread, c + 1)
                if not (isinstance(c, int) and c == 0):
                    dve.wait_ge(x16_ready, c)
                nc.vector.tensor_tensor(p16[:], misc[:], e4[:], ALU.mult).then_inc(p16_ready, 1)

            def lo_16(c):
                dve.wait_ge(x16_hi, c + 1)
                nc.vector.tensor_tensor(x16[F:2 * F], p16[F:2 * F], x16[F:2 * F].bitcast(F32),
                                        ALU.subtract).then_inc(x16_ready, 1)

            def zslice(layer, g):
                if isinstance(g, int):
                    return zacc[:, layer, g, :]
                return zacc[:, layer, bass.ds(g, 1), :].rearrange("p a c -> p (a c)")

            def add_z0(c, parity, g):
                dve.wait_ge(c0_ready, c + 1)
                dve.wait_ge(z0_added, c + 1)
                z = zslice(0, g)
                nc.vector.tensor_tensor(z, cspread[:, parity, 0, :], z, ALU.add).then_inc(z0_added, 1)

            def add_z1(c, parity, g, done):
                dve.wait_ge(step_done, done)
                dve.wait_ge(z1_added, c + 1)
                z = zslice(1, g)
                nc.vector.scalar_tensor_tensor(out=z, in0=acc1[:, parity], scalar=0.0, in1=z,
                                               op0=ALU.max, op1=ALU.add).then_inc(z1_added, 1)

            def iteration(k, base=None):
                def n(rate, const):
                    return const if base is None else base * (rate * 2) + const
                for j in range(LATE if k == LAST else PER):
                    s = HEAD + k * PER + j
                    product(s, n)
                    sub(s - DELTA, n)
                    j = place(s)
                    if j == DVE_16 and k < LAST:
                        product_16(n(1, k + 1))
                    if j == DVE_LO16 and k < LAST:
                        lo_16(n(1, k + 1))
                    if j == DVE_Z0 and k < LAST:
                        add_z0(n(1, k + 1), (k + 1) % 2, n(1, k + 1) // CPG)
                    if j == DVE_STAGE and k + 2 < CHUNKS:
                        stage_lo(n(1, k + 2))
                    if j == DVE_Z1 and k > 0:
                        add_z1(n(1, k - 1), (k - 1) % 2, n(1, k - 1) // CPG,
                               n(PER, last_step(k - 1) + 1))

            def static(rate, const):
                return const

            nc.vector.memset(stage[:, :, 2:4, :].bitcast(F32), 0.0).then_inc(stage_zero, 1)
            dve.wait_ge(f0_in, 32)
            nc.vector.tensor_tensor(w0a_raw[:, 0:4, :], w0a_raw[:, 0:4, :], w0b_raw,
                                    ALU.add).then_inc(f0_sum, 1)
            dve.wait_ge(split_hi, 1)
            nc.vector.tensor_tensor(f16[2 * F:3 * F], w0a_raw[2 * F:3 * F, 4, :],
                                    f16[2 * F:3 * F].bitcast(F32), ALU.subtract).then_inc(split_lo, 1)
            nc.vector.memset(f16[3 * F:4 * F].bitcast(F32), 0.0).then_inc(split_lo, 1)
            dve.wait_ge(split_hi, 2)
            nc.vector.tensor_tensor(f0l[:], w0a_raw[:, 0:4, :], f0h[:].bitcast(F32),
                                    ALU.subtract).then_inc(split_lo, 1)
            dve.wait_ge(split_hi, 3)
            nc.vector.tensor_tensor(f1l[:], w1_raw, f1h[:].bitcast(F32),
                                    ALU.subtract).then_inc(split_lo, 1)
            dve.wait_ge(consts_ready, 2)
            dve.wait_ge(split_lo, 4)
            nc.vector.memset(zacc[:, 0], 0.0).then_inc(z0_added, 1)
            nc.vector.memset(zacc[:, 1], 0.0).then_inc(z1_added, 1)

            stage_lo(0)
            product(0, static)
            product(1, static)
            product_16(0)
            sub(0, static)
            sub(1, static)
            lo_16(0)
            add_z0(0, 0, 0)
            stage_lo(1)
            for s in range(2, HEAD):
                product(s, static)
                if s - DELTA >= 2:
                    sub(s - DELTA, static)
            iteration(0)
            iteration(1)
            with dve.Fori(0, (CHUNKS - 4) // 2) as i:
                iteration(2, i)
                iteration(3, i)
            iteration(LAST - 1)
            iteration(LAST)
            for s in range(STEPS - DELTA, STEPS):
                sub(s, static)
            add_z1(LAST, LAST % 2, GROUPS - 1, STEPS)

            dve.wait_ge(z0_added, CHUNKS + 1)
            dve.wait_ge(z1_added, CHUNKS + 1)
            for half in range(2):
                for layer in range(2):
                    gs = slice(half * GROUPS // 2, (half + 1) * GROUPS // 2)
                    nc.vector.tensor_reduce(
                        zsum[:, layer, 512 * half:512 * (half + 1)].rearrange("p (g b) -> p g b", b=P),
                        zacc[:, layer, gs, :].rearrange("p g (d b) -> p g b d", b=P),
                        AX.X, ALU.add).then_inc(z_ready, 1)

        @block.tensor
        def _(pe):
            def spread_step(s, n):
                layer, c, item = decode(s)
                if FREED[s] is None:
                    return
                if FREED[s] >= 0:
                    pe.wait_ge(prod_ready, n(PER, FREED[s] + 1))
                if layer == 0 and item == 0:
                    pe.wait_ge(est_ready, n(1, c + 1))
                if layer == 0:
                    pe.matmul(espread[:, BANK[s]], shift[:, 2 * item], est[:, c % 2],
                              start=True, stop=True)
                    pe.matmul(espread[:, BANK[s] + 1], shift[:, 2 * item + 1], est[:, c % 2],
                              start=True, stop=True).then_inc(spread_ready, 1)
                else:
                    pe.matmul(espread[:, BANK[s]], pick[:, item // 2], est[:, c % 2],
                              start=True, stop=True).then_inc(spread_ready, 2)
                if layer == 0 and item == 1:
                    pe.wait_ge(e4_ready, n(1, c + 1))
                    pe.matmul(misc[:], shift[:, 4], est[:, c % 2], start=True,
                              stop=True).then_inc(s16_spread, 1)

            def products(s, n):
                layer, c, item = decode(s)
                x = kind(s)
                if x == FULL:
                    pe.wait_ge(prod_ready, n(PER, s + 1))
                else:
                    pe.wait_ge(lo_dve if x == DVE else lo_pool, n(RATE[x], before(s, x) + 1))
                if layer == 0 and item == 0 and not (s < HEAD):
                    pe.wait_ge(c0_ready, n(1, c))
                if layer == 1 and item == 0 and not (s < HEAD):
                    pe.wait_ge(z1_added, n(1, c))
                wh, wl = (f0h, f0l) if layer == 0 else (f1h, f1l)
                acc = acc0[:] if layer == 0 else acc1[:, c % 2]
                q = split_before(s)
                for i in range(2):
                    first, stop = item + i == 0, layer == 1 and item == PAIRS - 1 and i == 1
                    if x == FULL:
                        w = 2 * FULL_ITEMS.index(item) + i
                        mm = pe.matmul(acc, f1[:, w], prod[:, s % PRODS, i], start=first, stop=stop)
                        continue
                    w = 2 * (SPLIT_ITEMS.index(item) if layer else item) + i
                    h, l = hi[:, q % HIS, i], lo[:, q % LOS, i]
                    pe.matmul(acc, wl[:, w], h, start=first, stop=False)
                    pe.matmul(acc, wh[:, w], l, start=False, stop=False)
                    mm = pe.matmul(acc, wh[:, w], h, start=False, stop=stop)
                mm.then_inc(step_done, 1)

            def products_16(c):
                pe.wait_ge(x16_ready, c + 1)
                pe.matmul(acc0[:], f16[:], x16[:], start=False, stop=True).then_inc(acc0_done, 1)

            def turn(c):
                pe.wait_ge(staged, c + 1)
                if not (isinstance(c, int) and c == 0):
                    pe.wait_ge(p16_ready, c)
                for d in range(DPC):
                    src = stage[:, d].bitcast(F32).rearrange("p r x -> p (r x)")
                    t = pe.transpose(misc[:, d * P:(d + 1) * P], src, ident[:])
                t.then_inc(turned, 1)

            def spread_e4(c, parity):
                pe.wait_ge(est_ready, c + 1)
                pe.matmul(misc[:], shift[:, 5], est[:, parity], start=True,
                          stop=True).then_inc(e4_spread, 1)

            def iteration(k, base=None):
                def n(rate, const):
                    return const if base is None else base * (rate * 2) + const
                for j in range(LATE if k == LAST else PER):
                    s = HEAD + k * PER + j
                    if s + AHEAD < STEPS:
                        spread_step(s + AHEAD, n)
                    products(s, n)
                    j = place(s)
                    if j == PE_16 and k < LAST:
                        products_16(n(1, k + 1))
                    if j == PE_TURN and k + 2 < CHUNKS:
                        turn(n(1, k + 2))
                    if j == PE_E4 and k + 2 < CHUNKS:
                        spread_e4(n(1, k + 2), k % 2)

            def static(rate, const):
                return const

            pe.wait_ge(const_in, 32)
            pe.wait_ge(consts_ready, 2)
            pe.wait_ge(stage_zero, 1)
            turn(0)
            spread_e4(0, 0)
            spread_step(0, static)
            spread_step(1, static)
            pe.wait_ge(f1_full_in, 16)
            pe.wait_ge(split_hi, 3)
            pe.wait_ge(split_lo, 4)
            products(0, static)
            products(1, static)
            products_16(0)
            turn(1)
            spread_e4(1, 1)
            for s in range(2, 2 + AHEAD):
                spread_step(s, static)
            for s in range(2, HEAD):
                spread_step(s + AHEAD, static)
                products(s, static)
            with pe.Fori(0, (CHUNKS - 2) // 2) as i:
                iteration(0, i)
                iteration(1, i)
            iteration(LAST - 1)
            iteration(LAST)

            pe.wait_ge(tower_in, TOWER_IN)
            for half in range(2):
                cols = slice(512 * half, 512 * (half + 1))
                pe.wait_ge(z_ready, 2 * half + 2)
                for m in range(H1 // P):
                    ms = slice(m * P, (m + 1) * P)
                    if half:
                        pe.wait_ge(h1_ready, m + 1)
                    o = espread[:, m]
                    pe.matmul(o, wt1_sb[:, 0, ms], zsum[:, 0, cols], start=True, stop=False)
                    pe.matmul(o, wt1_sb[:, 1, ms], zsum[:, 1, cols], start=False, stop=False)
                    pe.matmul(o, wt1d_sb[:, ms], dense_sb[:, cols], start=False,
                              stop=True).then_inc(h1_sum, 1)
                for m in range(H2 // P):
                    if half:
                        pe.wait_ge(h2_ready, m + 1)
                    for t in range(H1 // P):
                        if m == 0:
                            pe.wait_ge(h1_ready, 4 * half + t + 1)
                        mm = pe.matmul(acc1[:, m], wt2_sb[:, t, m * P:(m + 1) * P], h1[:, t],
                                       start=(t == 0), stop=(t == H1 // P - 1))
                    mm.then_inc(h2_sum, 1)
                if half:
                    pe.wait_ge(y_ready, 1)
                for t in range(H2 // P):
                    pe.wait_ge(h2_ready, 2 * half + t + 1)
                    mm = pe.matmul(acc0[0:1, :], wt3_sb[:, t:t + 1], h2[:, t],
                                   start=(t == 0), stop=(t == H2 // P - 1))
                mm.then_inc(y_sum, 1)


def layout_constants():
    k, col = np.arange(P), np.arange(P)
    takes = [HPT * hg + col // MPT for hg in range(HG)]
    takes += [(col % F + 4 * t + col // F) % F for t in range(TILES0)]
    takes += [(col % F + 16) % F, col % F]
    out = np.zeros((P, (HG + 7) * P), np.float32)
    for t, f in enumerate(takes):
        out[:, t * P:(t + 1) * P] = (k[:, None] % F == f[None, :]) & (k[:, None] < 2 * F)
    out[:, (HG + 6) * P:] = np.eye(P)
    return out


def kernel(**inputs):
    import concourse.bacc as bacc
    from concourse.bass_utils import run_bass_kernel_spmd

    x = {k: np.asarray(v) for k, v in inputs.items()}
    f0 = x["L0_rec_filter_0"][0].reshape(F, F, N)
    f = np.arange(F)
    w0a = np.zeros((P, 5, N), np.float32)
    w0b = np.zeros((P, 4, N), np.float32)
    for s in range(16):
        r = slice((s % 4) * F, (s % 4 + 1) * F)
        w0a[r, s // 4] = f0[f, (f + s) % F]
        if s:
            w0b[r, s // 4] = f0[(f + s) % F, f]
    for r in range(4):
        w0a[r * F:(r + 1) * F, 4] = f0[f, (f + 16) % F]
    w1 = x["L0_rec_filter_1"][0].reshape(HG, HPT, MG, MPT, N)
    w1 = np.stack([w1[:, h][:, (np.arange(MG) + h) % MG] for h in range(HPT)])
    w1 = w1.transpose(0, 3, 1, 2, 4)
    w1 = w1.reshape(P, PAIRS, 2, N)[:, SPLIT_ITEMS + FULL_ITEMS].reshape(P, HG * MG, N)
    arrays = {f"tbl_{i}": x[f"tbl_{i}"] for i in range(F)}
    arrays |= {
        "ids": x["ids"], "w0a": w0a, "w0b": w0b, "w1": w1, "consts": layout_constants(),
        "dense_t": np.ascontiguousarray(x["dense_ctx"].T),
        "wt1": x["W_top1"][:2 * N], "wt1d": x["W_top1"][2 * N:], "wt2": x["W_top2"],
        "wt3": np.ascontiguousarray(x["W_top3"].reshape(H2 // P, P).T),
        "bt1": np.ascontiguousarray(x["b_top1"].reshape(H1 // P, P).T),
        "bt2": np.ascontiguousarray(x["b_top2"].reshape(H2 // P, P).T),
    }
    arrays = {f"in_{k}": np.ascontiguousarray(v) for k, v in arrays.items()}
    nc = bacc.Bacc("TRN2", target_bir_lowering=False, num_devices=1)
    ap = {k: nc.dram_tensor(k, v.shape, mybir.dt.from_np(v.dtype), kind="ExternalInput").ap()
          for k, v in arrays.items()}
    out = nc.dram_tensor("out", (B,), F32, kind="ExternalOutput").ap()
    build(nc, [ap[f"in_tbl_{i}"] for i in range(F)], ap["in_ids"], ap["in_w0a"], ap["in_w0b"],
          ap["in_w1"], ap["in_consts"], ap["in_dense_t"], ap["in_wt1"], ap["in_wt1d"], ap["in_wt2"],
          ap["in_wt3"], ap["in_bt1"], ap["in_bt2"], out)
    r = run_bass_kernel_spmd(nc, [arrays], core_ids=[0])
    return r.results[0]["out"].reshape(B, 1)
```

```python
from contextlib import ExitStack

import numpy as np

import concourse.bass as bass
from concourse import mybir

ALU = mybir.AluOpType
ACT = mybir.ActivationFunctionType
AX = mybir.AxisListType
F32 = mybir.dt.float32
F32R = mybir.dt.float32r
I32 = mybir.dt.int32

P = 128
B, F, D, N = 1024, 32, 32, 128
GROUPS = B // P
CPG = 8
DPC = D // CPG
COLS = DPC * P
CHUNKS = GROUPS * CPG
LAST = CHUNKS - 1
TILES0 = 4
DENSE, H1, H2 = 16, 512, 256

HPB = COLS // N
BANKS1 = F // HPB * DPC
OWNER = "DADADADAADADADADAADADADADADAADAA"
DVE_BANKS, ACT_BANKS = OWNER.count("D"), OWNER.count("A")
MACS = DVE_BANKS * HPB
ADDS = (ACT_BANKS - DPC) // 2
RING = 6
SUMS = 4
assert len(OWNER) == BANKS1 and ACT_BANKS % 2 == 0

PE_AT = (0, 2, 4, 6)
PE_TILE, PE_16, PE_TURN = (12, 14, 16, 18), 20, 22
ACT_HI, ACT_16, ACT_STAGE, ACT_C0, ACT_EST = (3, 5, 7, 10), 10, 13, 21, 23
DVE_PROD, DVE_P16, DVE_LO, DVE_LO16 = (0, 2, 4, 6), 8, (7, 10, 12, 14), 16
DVE_C0, DVE_Z0, DVE_EST, DVE_Z1 = 23, 26, 27, 28
DVE_HALVE = 15
POOL_ORDER = "-01ab23456"
TAIL_Z1, TAIL_Z0, TAIL_PE, TAIL_ACT = 2, 20, 16, 21
TAIL_DENSE = (3, 26)

_twos = [(HPB * x, 2 * p) for x in range(F // HPB) for p in range(DPC // 2)]
_of_act = [(h, d + x) for h, d in _twos[:ACT_BANKS // 2] for x in range(2)]
_of_dve = [(h, d + x) for h, d in _twos[ACT_BANKS // 2:] for x in range(2)]
BANK1, RANK = [], []
for _i, _who in enumerate(OWNER):
    RANK.append(OWNER[:_i].count(_who))
    BANK1.append((_of_dve if _who == "D" else _of_act)[RANK[-1]])


FILLS, PLACE = [], {}


def _fill(layer, c, i):
    PLACE[layer, c, i] = len(FILLS)
    FILLS.append((layer, c, i))


for _i in range(TILES0):
    _fill(0, 0, _i)
for _c in range(CHUNKS):
    for _i in range(BANKS1):
        for _j in range(TILES0):
            if _i == PE_AT[_j] and _c < LAST:
                _fill(0, _c + 1, _j)
        _fill(1, _c, _i)


def build(nc, tables, ids, w0a, w0b, w1, consts, dense_t, wt1, wt1d, wt2, wt3, bt1, bt2, out):
    with ExitStack() as ctx:
        def sb(name, shape, dt=F32):
            return ctx.enter_context(nc.sbuf_tensor(name, shape, dt))

        def sem(name):
            return ctx.enter_context(nc.semaphore(name))

        ring = ctx.enter_context(nc.psum_tensor("ring", [P, RING, COLS], F32))
        acc0 = ctx.enter_context(nc.psum_tensor("acc0", [P, COLS], F32))
        misc = ctx.enter_context(nc.psum_tensor("misc", [P, COLS], F32))

        f1h = sb("f1h", [P, F, N], F32R)
        f1l = sb("f1l", [P, F, N], F32R)
        f0h = sb("f0h", [P, TILES0, N], F32R)
        f0l = sb("f0l", [P, TILES0, N], F32R)
        f16 = sb("f16", [P, N], F32R)
        shift = sb("shift", [P, 5, P], F32R)
        ident = sb("ident", [P, P])

        ids_sb = sb("ids_sb", [P, GROUPS, F], I32)
        ids_now = sb("ids_now", [P, F], I32)
        rows = sb("rows", [P, F, D])
        emb = sb("emb", [P, 2, F, D])
        mark = sb("mark", [P, 1])
        stage = sb("stage", [P, DPC, 4, F])
        ecol = sb("ecol", [P, 4, F, DPC])
        est = sb("est", [P, 2, COLS], F32R)
        e4 = sb("e4", [P, COLS])

        prod = sb("prod", [P, TILES0, COLS])
        hi = sb("hi", [P, TILES0, COLS], F32R)
        lo = sb("lo", [P, TILES0, COLS], F32R)
        p16 = sb("p16", [P, COLS])
        x16 = sb("x16", [P, COLS], F32R)

        c0h = sb("c0h", [P, 2, COLS], F32R)
        c0l = sb("c0l", [P, 2, COLS], F32R)
        acc_dve = sb("acc_dve", [P, 2, DPC, 2, N])
        acc_pool = sb("acc_pool", [P, 2, DPC, HPB, N])
        scaled_t = sb("scaled_t", [P, SUMS, 2, HPB, N])
        c1 = sb("c1", [P, 2, DPC, N])

        z0 = sb("z0", [P, GROUPS, COLS])
        z1 = sb("z1", [P, GROUPS, COLS])
        wt1_sb = sb("wt1_sb", [P, 2, H1])
        wt2_sb = sb("wt2_sb", [P, H1 // P, H2])
        wt3_sb = sb("wt3_sb", [P, H2 // P])
        bt1_sb = sb("bt1_sb", [P, H1 // P])
        bt2_sb = sb("bt2_sb", [P, H2 // P])
        z1_rows = sb("z1_rows", [P, GROUPS, N])
        h1 = sb("h1", [P, H1 // P, COLS])
        h2 = sb("h2", [P, H2 // P, COLS])
        y_sb = sb("y_sb", [1, B])

        w1_raw = z0[:].rearrange("p g c -> p (g c)").rearrange("p (h n) -> p h n", n=N)
        raw = z1[:].rearrange("p g c -> p (g c)")
        w0a_raw = raw[:, 0:5 * N].rearrange("p (t n) -> p t n", n=N)
        w0b_raw = raw[:, 5 * N:9 * N].rearrange("p (t n) -> p t n", n=N)
        shift_raw = raw[:, 9 * N:9 * N + 5 * P].rearrange("p (t n) -> p t n", n=P)
        old = emb[:].rearrange("p a f d -> p (a f d)")
        dense_sb, wt1d_sb = old[:, 0:B], old[:, B:B + H1]
        old = hi[:].rearrange("p a c -> p (a c)")
        dense_r, wt1d_r = old[:, 0:B], old[:, B:B + H1]
        zsum = prod[:].rearrange("p a c -> p (a c)").rearrange("p (l b) -> p l b", l=2)

        ids_in, f1_in, f0_in, const_in, tower_in = (
            sem(x) for x in ("ids_in", "f1_in", "f0_in", "const_in", "tower_in"))
        split_hi, f0_sum, split_lo, shift_ready = (
            sem(x) for x in ("split_hi", "f0_sum", "split_lo", "shift_ready"))
        ids_ready, gathered, rows_kept, emb_ready = (
            sem(x) for x in ("ids_ready", "gathered", "rows_kept", "emb_ready"))
        ecol_ready, staged, turned, e4_ready, est_hi, est_ready = (
            sem(x) for x in ("ecol_ready", "staged", "turned", "e4_ready", "est_hi", "est_ready"))
        spread_ready, prod_ready, hi_ready, lo_ready = (
            sem(x) for x in ("spread_ready", "prod_ready", "hi_ready", "lo_ready"))
        s16_spread, p16_ready, x16_hi, x16_ready, acc0_done, c0h_ready, c0l_ready, z0_added = (
            sem(x) for x in ("s16_spread", "p16_ready", "x16_hi", "x16_ready", "acc0_done", "c0h_ready",
                             "c0l_ready", "z0_added"))
        filled, mac_done, scaled, pool_added, halved, joined, c1_ready, z1_added = (
            sem(x) for x in ("filled", "mac_done", "scaled", "pool_added", "halved", "joined", "c1_ready",
                             "z1_added"))
        z0_ready, z1_ready, z1_turned, zsum_ready = (
            sem(x) for x in ("z0_ready", "z1_ready", "z1_turned", "zsum_ready"))
        dense_hi, dense_ready = sem("dense_hi"), sem("dense_ready")
        h1_sum, h1_ready, h2_sum, h2_ready, y_sum, y_ready, stored = (
            sem(x) for x in ("h1_sum", "h1_ready", "h2_sum", "h2_ready", "y_sum", "y_ready", "stored"))
        TOWER_IN = 16 * 7

        def emb_chunk(c):
            g = c // CPG
            if isinstance(c, int):
                return emb[:, g % 2, :, c % CPG * DPC:(c % CPG + 1) * DPC]
            return emb[:, bass.ds(g % 2, 1), :, bass.ds((c % CPG) * DPC, DPC)].rearrange(
                "p a f d -> p (a f) d")

        block = ctx.enter_context(nc.Block())

        @block.sync
        def _(sp):
            sp.dma_start(ids_sb[:], ids.rearrange("(g p) f -> p g f", p=P)).then_inc(ids_in, 16)
            sp.dma_start(shift_raw, consts[:, 0:5 * P]).then_inc(const_in, 16)
            sp.dma_start(ident[:], consts[:, 5 * P:]).then_inc(const_in, 16)
            sp.dma_start(w0a_raw, w0a).then_inc(f0_in, 16)
            sp.dma_start(w0b_raw, w0b).then_inc(f0_in, 16)
            sp.dma_start(w1_raw, w1).then_inc(f1_in, 16)
            sp.dma_start(wt1_sb[:], wt1.rearrange("(t p) n -> p t n", p=P)).then_inc(tower_in, 16)
            sp.dma_start(wt2_sb[:], wt2.rearrange("(t p) n -> p t n", p=P)).then_inc(tower_in, 16)
            sp.dma_start(wt3_sb[:], wt3).then_inc(tower_in, 16)
            sp.dma_start(bt1_sb[:], bt1).then_inc(tower_in, 16)
            sp.dma_start(bt2_sb[:], bt2).then_inc(tower_in, 16)
            sp.wait_ge(staged, CHUNKS)
            sp.dma_start(wt1d_sb, wt1d).then_inc(tower_in, 16)
            sp.dma_start(dense_sb, dense_t).then_inc(tower_in, 16)
            sp.wait_ge(y_ready, 2)
            sp.dma_start(out.unsqueeze(0), y_sb[:]).then_inc(stored, 16)
            sp.wait_ge(stored, 16)

        @block.gpsimd
        def _(pool):
            def load_ids(g):
                nc.gpsimd.tensor_copy(ids_now[:], ids_sb[:, g, :] if isinstance(g, int)
                                      else ids_sb[:, bass.ds(g, 1), :].rearrange("p a f -> p (a f)")
                                      ).then_inc(ids_ready, 1)
                if not (isinstance(g, int) and g == 0):
                    tell_emb()
                pool.wait_ge(ids_ready, g + 1)

            def gather(f, to=rows[:]):
                nc.gpsimd.indirect_dma_start(
                    to[:, f, :], None, tables[f],
                    bass.IndirectOffsetOnAxis(ap=ids_now[:, f:f + 1], axis=0)).then_inc(gathered, 16)

            def tell_emb():
                nc.gpsimd.memset(mark[:], 0.0).then_inc(emb_ready, 1)

            def keep_rows(g, parity):
                pool.wait_ge(gathered, (g + 1) * (16 * F))
                if not (isinstance(g, int) and g < 2):
                    pool.wait_ge(staged, (g - 1) * CPG)
                half = emb[:, parity] if isinstance(parity, int) else \
                    emb[:, bass.ds(parity, 1)].rearrange("p a f d -> p (a f) d")
                nc.gpsimd.dma_start(half, rows[:]).then_inc(rows_kept, 16)

            def add(c, j, n):
                at = ADDS * c + j
                p = j % 2
                pool.wait_ge(scaled, n(ACT_BANKS, ACT_BANKS * c + DPC + 2 * j + 2))
                if j >= 2:
                    pool.wait_ge(pool_added, n(ADDS, at - 1))
                s = acc_pool[:, c % 2, 2 * p:2 * p + 2]
                nc.gpsimd.tensor_tensor(s, s, scaled_t[:, at % SUMS], ALU.add).then_inc(pool_added, 1)

            def finish(c, part, n):
                s = acc_pool[:, c % 2]
                if part == 0:
                    pool.wait_ge(mac_done, n(MACS, MACS * (c + 1)))
                    pool.wait_ge(halved, n(1, c + 1))
                    nc.gpsimd.tensor_tensor(s[:, :, 0:2], s[:, :, 0:2], acc_dve[:, c % 2],
                                            ALU.add).then_inc(joined, 1)
                else:
                    pool.wait_ge(joined, n(1, c + 1))
                    if c >= 2:
                        pool.wait_ge(z1_added, n(1, c))
                    nc.gpsimd.tensor_tensor(c1[:, c % 2], s[:, :, 0], s[:, :, 1],
                                            ALU.add).then_inc(c1_ready, 1)

            def iteration(k, fields, base=None, per=0):
                def n(rate, const):
                    return const if base is None else base * (rate * per) + const
                for i, what in enumerate(POOL_ORDER):
                    if what >= "a":
                        if k > 0:
                            finish(k - 1, "ab".index(what), n)
                    elif what != "-":
                        add(k, int(what), n)
                    m = len(POOL_ORDER)
                    for f in fields[len(fields) * i // m:len(fields) * (i + 1) // m]:
                        gather(f)

            pool.wait_ge(ids_in, 16)
            load_ids(0)
            for f in range(F):
                gather(f, emb[:, 0])
            pool.wait_ge(gathered, 16 * F)
            load_ids(1)
            for k in range(5):
                iteration(k, range(F * k // 5, F * (k + 1) // 5))
            keep_rows(1, 1)
            iteration(5, range(0))
            with pool.Fori(0, GROUPS - 2) as i:
                pool.wait_ge(rows_kept, i * 16 + 16)
                load_ids(i + 2)
                for m in range(CPG):
                    iteration(6 + m, range(F * m // 7, F * (m + 1) // 7) if m < 7 else range(0), i, CPG)
                    if m == 6:
                        keep_rows(i + 2, i % 2)
            pool.wait_ge(rows_kept, 16 * (GROUPS - 1))
            tell_emb()
            for k in range(6 + CPG * (GROUPS - 2), CHUNKS):
                iteration(k, range(0))
            for part in range(2):
                finish(LAST, part, lambda rate, const: const)

        @block.scalar
        def _(act):
            def stage_chunk(c):
                static = isinstance(c, int)
                act.wait_ge(emb_ready, c // CPG + 1)
                if not (static and c == 0):
                    act.wait_ge(turned, c)
                e = emb_chunk(c)
                slot = ecol[:, c % 4] if static else ecol[:, bass.ds(c % 4, 1)].rearrange(
                    "p a f d -> p (a f) d")
                nc.scalar.activation(slot, e, ACT.Copy).then_inc(ecol_ready, 1)
                nc.scalar.activation(stage[:], e.rearrange("p f d -> p d f").unsqueeze(2).to_broadcast(
                    [P, DPC, 4, F]), ACT.Copy).then_inc(staged, 1)

            def store_e4(c, parity):
                act.wait_ge(turned, c + 1)
                nc.scalar.activation(e4[:], misc[:], ACT.Copy).then_inc(e4_ready, 1)
                nc.scalar.activation(est[:, parity], misc[:], ACT.Copy).then_inc(est_hi, 1)

            def round_16(c):
                act.wait_ge(p16_ready, c + 1)
                if not (isinstance(c, int) and c == 0):
                    act.wait_ge(acc0_done, c)
                nc.scalar.activation(x16[:], p16[:], ACT.Copy).then_inc(x16_hi, 1)

            def round_c0(c, parity):
                act.wait_ge(acc0_done, c + 1)
                nc.scalar.activation(c0h[:, parity], acc0[:], ACT.Relu).then_inc(c0h_ready, 1)

            def round_tile(c, item, n):
                act.wait_ge(prod_ready, n(TILES0, TILES0 * c + item + 1))
                nc.scalar.activation(hi[:, item], prod[:, item], ACT.Copy).then_inc(hi_ready, 1)

            def scale(c, i, n):
                (h, d), j = BANK1[i], RANK[i]
                act.wait_ge(filled, n(BANKS1, BANKS1 * c + i + 1))
                if j < DPC:
                    if j == 0 and c >= 2:
                        act.wait_ge(c1_ready, n(1, c - 1))
                    if j == 0:
                        act.wait_ge(ecol_ready, n(1, c + 1))
                    dst = acc_pool[:, c % 2, d]
                else:
                    at = ADDS * c + (j - DPC) // 2
                    if at >= SUMS and d % 2 == 0:
                        act.wait_ge(pool_added, n(ADDS, at - SUMS + 1))
                    dst = scaled_t[:, at % SUMS, d % 2]
                bank = PLACE[1, c, i] % RING
                for x in range(HPB):
                    one = nc.scalar.activation(dst[:, x], ring[:, bank, x * N:(x + 1) * N], ACT.Copy,
                                               scale=ecol[:, c % 4, h + x, d:d + 1])
                one.then_inc(scaled, 1)

            def round_dense():
                act.wait_ge(tower_in, TOWER_IN)
                nc.scalar.activation(dense_r, dense_sb, ACT.Copy).then_inc(dense_hi, 1)
                nc.scalar.activation(wt1d_r, wt1d_sb, ACT.Copy).then_inc(dense_hi, 1)

            def keep_turned(half):
                act.wait_ge(z1_turned, half + 1)
                nc.scalar.activation(zsum[:, 1, 512 * half:512 * (half + 1)], misc[:],
                                     ACT.Copy).then_inc(zsum_ready, 1)

            def iteration(k, base=None):
                def n(rate, const):
                    return const if base is None else base * (rate * 4) + const
                for j in range(BANKS1):
                    if OWNER[j] == "A":
                        scale(k, j, n)
                    for item in range(TILES0):
                        if j == ACT_HI[item] and k < LAST:
                            round_tile(k + 1, item, n)
                    if j == ACT_16 and k < LAST:
                        round_16(n(1, k + 1))
                    if j == ACT_STAGE and k + 2 < CHUNKS:
                        stage_chunk(n(1, k + 2))
                    if j == ACT_C0 and k < LAST:
                        round_c0(n(1, k + 1), (k + 1) % 2)
                    if j == ACT_EST and k + 2 < CHUNKS:
                        store_e4(n(1, k + 2), k % 2)
                    if j == TAIL_DENSE[0] and k == LAST:
                        round_dense()
                    if j == TAIL_ACT and k == LAST:
                        keep_turned(0)

            def static(rate, const):
                return const

            act.wait_ge(const_in, 32)
            nc.scalar.activation(shift[:], shift_raw, ACT.Copy).then_inc(shift_ready, 1)
            act.wait_ge(f0_in, 32)
            nc.scalar.activation(f16[:], w0a_raw[:, 4, :], ACT.Copy).then_inc(split_hi, 1)
            act.wait_ge(f0_sum, 1)
            nc.scalar.activation(f0h[:], w0a_raw[:, 0:4, :], ACT.Copy).then_inc(split_hi, 1)
            act.wait_ge(f1_in, 16)
            nc.scalar.activation(f1h[:], w1_raw, ACT.Copy).then_inc(split_hi, 1)

            stage_chunk(0)
            store_e4(0, 0)
            stage_chunk(1)
            for item in range(TILES0):
                round_tile(0, item, static)
            round_16(0)
            round_c0(0, 0)
            store_e4(1, 1)
            iteration(0)
            iteration(1)
            with act.Fori(0, (CHUNKS - 4) // 4) as i:
                for k in range(2, 6):
                    iteration(k, i)
            iteration(LAST - 1)
            iteration(LAST)

            act.wait_ge(tower_in, TOWER_IN)
            for half in range(2):
                if half:
                    keep_turned(1)
                for m in range(H1 // P):
                    act.wait_ge(h1_sum, 4 * half + m + 1)
                    if half:
                        act.wait_ge(h2_sum, 2)
                    nc.scalar.activation(h1[:, m], ring[:, m], ACT.Relu,
                                         bias=bt1_sb[:, m:m + 1]).then_inc(h1_ready, 1)
                for m in range(H2 // P):
                    act.wait_ge(h2_sum, 2 * half + m + 1)
                    if half:
                        act.wait_ge(y_sum, 1)
                    nc.scalar.activation(h2[:, m], ring[:, H1 // P + m], ACT.Relu,
                                         bias=bt2_sb[:, m:m + 1]).then_inc(h2_ready, 1)
                act.wait_ge(y_sum, half + 1)
                nc.scalar.activation(y_sb[:, 512 * half:512 * (half + 1)], acc0[0:1, :],
                                     ACT.Copy).then_inc(y_ready, 1)

        @block.vector
        def _(dve):
            def product(c, item, n):
                dve.wait_ge(spread_ready, n(TILES0, TILES0 * c + item + 1))
                if item == 0:
                    dve.wait_ge(e4_ready, n(1, c + 1))
                    if c > 0:
                        dve.wait_ge(acc0_done, n(1, c))
                bank = PLACE[0, c, item] % RING
                nc.vector.tensor_tensor(prod[:, item], ring[:, bank], e4[:],
                                        ALU.mult).then_inc(prod_ready, 1)

            def sub(c, item, n):
                dve.wait_ge(hi_ready, n(TILES0, TILES0 * c + item + 1))
                nc.vector.tensor_tensor(lo[:, item], prod[:, item], hi[:, item].bitcast(F32),
                                        ALU.subtract).then_inc(lo_ready, 1)

            def low_est(c, parity):
                dve.wait_ge(est_hi, c + 1)
                r = est[F:2 * F, parity]
                nc.vector.tensor_tensor(r, e4[F:2 * F], r.bitcast(F32), ALU.subtract).then_inc(est_ready, 1)

            def product_16(c):
                dve.wait_ge(s16_spread, c + 1)
                if not (isinstance(c, int) and c == 0):
                    dve.wait_ge(x16_ready, c)
                nc.vector.tensor_tensor(p16[:], misc[:], e4[:], ALU.mult).then_inc(p16_ready, 1)

            def lo_16(c):
                dve.wait_ge(x16_hi, c + 1)
                nc.vector.tensor_tensor(x16[F:2 * F], p16[F:2 * F], x16[F:2 * F].bitcast(F32),
                                        ALU.subtract).then_inc(x16_ready, 1)

            def of_group(z, g):
                return z[:, g] if isinstance(g, int) else \
                    z[:, bass.ds(g, 1), :].rearrange("p a c -> p (a c)")

            def low_c0(c, parity):
                dve.wait_ge(c0h_ready, c + 1)
                nc.vector.scalar_tensor_tensor(
                    out=c0l[:, parity], in0=acc0[:], scalar=0.0, in1=c0h[:, parity].bitcast(F32),
                    op0=ALU.max, op1=ALU.subtract).then_inc(c0l_ready, 1)

            def add_z0(c, g):
                dve.wait_ge(z0_added, c + 1)
                z = of_group(z0, g)
                nc.vector.scalar_tensor_tensor(out=z, in0=acc0[:], scalar=0.0, in1=z,
                                               op0=ALU.max, op1=ALU.add).then_inc(z0_added, 1)

            def add_z1(c, parity, g):
                dve.wait_ge(c1_ready, c + 1)
                dve.wait_ge(z1_added, c + 1)
                z = of_group(z1, g)
                nc.vector.scalar_tensor_tensor(
                    out=z, in0=c1[:, parity].rearrange("p d n -> p (d n)"), scalar=0.0, in1=z,
                    op0=ALU.max, op1=ALU.add).then_inc(z1_added, 1)

            def mac(c, i, n):
                (h, d), j = BANK1[i], RANK[i]
                dve.wait_ge(filled, n(BANKS1, BANKS1 * c + i + 1))
                if j == 0 and c >= 2:
                    dve.wait_ge(c1_ready, n(1, c - 1))
                bank = PLACE[1, c, i] % RING
                for x in range(HPB):
                    acc = acc_dve[:, c % 2, d, x % 2]
                    t, e = ring[:, bank, x * N:(x + 1) * N], ecol[:, c % 4, h + x, d:d + 1]
                    if x >= 2:
                        dve.wait_ge(mac_done, n(MACS, MACS * c + HPB * j + x - 1))
                    if j < DPC and x < 2:
                        op = nc.vector.tensor_scalar(acc, t, e, None, ALU.mult)
                    else:
                        op = nc.vector.scalar_tensor_tensor(out=acc, in0=t, scalar=e, in1=acc,
                                                            op0=ALU.mult, op1=ALU.add)
                    op.then_inc(mac_done, 1)

            def halve(c, n):
                dve.wait_ge(pool_added, n(ADDS, ADDS * (c + 1)))
                s = acc_pool[:, c % 2]
                nc.vector.tensor_tensor(s[:, :, 0:2], s[:, :, 0:2], s[:, :, 2:4],
                                        ALU.add).then_inc(halved, 1)

            def low_dense():
                for rows_lo, raw, split, count in ((slice(32, 64), dense_sb, dense_r, 1),
                                                   (slice(64, 96), wt1d_sb, wt1d_r, 2)):
                    dve.wait_ge(dense_hi, count)
                    nc.vector.tensor_tensor(split[rows_lo], raw[rows_lo], split[rows_lo].bitcast(F32),
                                            ALU.subtract).then_inc(dense_ready, 1)

            def reduce_z1(g0, g1):
                dve.wait_ge(z1_added, CPG * g1 + 1)
                nc.vector.tensor_reduce(z1_rows[:, g0:g1],
                                        z1[:, g0:g1].rearrange("p g (d n) -> p g n d", n=N),
                                        AX.X, ALU.add).then_inc(z1_ready, 1)

            def reduce_z0(g0, g1):
                dve.wait_ge(z0_added, CHUNKS + 1)
                nc.vector.tensor_reduce(
                    zsum[:, 0, P * g0:P * g1].rearrange("p (g b) -> p g b", b=P),
                    z0[:, g0:g1].rearrange("p g (d b) -> p g b d", b=P),
                    AX.X, ALU.add).then_inc(z0_ready, 1)

            def iteration(k, base=None):
                def n(rate, const):
                    return const if base is None else base * (rate * 4) + const
                for j in range(BANKS1):
                    if OWNER[j] == "D":
                        mac(k, j, n)
                    if j == DVE_HALVE and k > 0:
                        halve(k - 1, n)
                    for item in range(TILES0):
                        if j == DVE_PROD[item] and k < LAST:
                            product(k + 1, item, n)
                    if j == DVE_P16 and k < LAST:
                        product_16(n(1, k + 1))
                    for item in range(TILES0):
                        if j == DVE_LO[item] and k < LAST:
                            sub(k + 1, item, n)
                    if j == DVE_LO16 and k < LAST:
                        lo_16(n(1, k + 1))
                    if j == DVE_EST and k + 2 < CHUNKS:
                        low_est(n(1, k + 2), k % 2)
                    if j == DVE_C0 and k < LAST:
                        low_c0(n(1, k + 1), (k + 1) % 2)
                    if j == DVE_Z0 and k < LAST:
                        add_z0(n(1, k + 1), n(1, k + 1) // CPG)
                    if j == DVE_Z1 and k > 0:
                        add_z1(n(1, k - 1), (k - 1) % 2, n(1, k - 1) // CPG)
                    if j == TAIL_DENSE[1] and k == LAST:
                        low_dense()
                    if j == TAIL_Z1 and k == LAST:
                        reduce_z1(0, GROUPS // 2)
                    if j == TAIL_Z0 and k == LAST:
                        reduce_z0(0, GROUPS // 2)

            def static(rate, const):
                return const

            dve.wait_ge(f0_in, 32)
            nc.vector.tensor_tensor(w0a_raw[:, 0:4, :], w0a_raw[:, 0:4, :], w0b_raw,
                                    ALU.add).then_inc(f0_sum, 1)
            dve.wait_ge(split_hi, 1)
            nc.vector.tensor_tensor(f16[2 * F:3 * F], w0a_raw[2 * F:3 * F, 4, :],
                                    f16[2 * F:3 * F].bitcast(F32), ALU.subtract).then_inc(split_lo, 1)
            nc.vector.memset(f16[3 * F:4 * F].bitcast(F32), 0.0).then_inc(split_lo, 1)
            dve.wait_ge(split_hi, 2)
            nc.vector.tensor_tensor(f0l[:], w0a_raw[:, 0:4, :], f0h[:].bitcast(F32),
                                    ALU.subtract).then_inc(split_lo, 1)
            dve.wait_ge(split_hi, 3)
            nc.vector.tensor_tensor(f1l[:], w1_raw, f1h[:].bitcast(F32),
                                    ALU.subtract).then_inc(split_lo, 1)
            dve.wait_ge(shift_ready, 1)
            dve.wait_ge(split_lo, 4)
            nc.vector.memset(z0[:], 0.0).then_inc(z0_added, 1)
            nc.vector.memset(z1[:], 0.0).then_inc(z1_added, 1)

            low_est(0, 0)
            product(0, 0, static)
            for item in range(1, TILES0):
                product(0, item, static)
                sub(0, item - 1, static)
            product_16(0)
            sub(0, TILES0 - 1, static)
            lo_16(0)
            low_c0(0, 0)
            add_z0(0, 0)
            low_est(1, 1)
            iteration(0)
            iteration(1)
            with dve.Fori(0, (CHUNKS - 4) // 4) as i:
                for k in range(2, 6):
                    iteration(k, i)
            iteration(LAST - 1)
            iteration(LAST)
            halve(LAST, static)
            reduce_z1(GROUPS // 2, GROUPS - 1)
            reduce_z0(GROUPS // 2, GROUPS)
            add_z1(LAST, LAST % 2, GROUPS - 1)
            reduce_z1(GROUPS - 1, GROUPS)

        @block.tensor
        def _(pe):
            def wait_bank(at, n):
                if at < RING:
                    return
                layer, c, i = FILLS[at - RING]
                if layer == 0:
                    pe.wait_ge(prod_ready, n(TILES0, TILES0 * c + i + 1))
                elif OWNER[i] == "D":
                    pe.wait_ge(mac_done, n(MACS, MACS * c + HPB * (RANK[i] + 1)))
                else:
                    pe.wait_ge(scaled, n(ACT_BANKS, ACT_BANKS * c + RANK[i] + 1))

            def spread_tile(c, item, n):
                at = PLACE[0, c, item]
                if item == 0:
                    pe.wait_ge(est_ready, n(1, c + 1))
                wait_bank(at, n)
                pe.matmul(ring[:, at % RING], shift[:, item], est[:, c % 2],
                          start=True, stop=True).then_inc(spread_ready, 1)
                if item == TILES0 - 1:
                    pe.matmul(misc[:], shift[:, 4], est[:, c % 2], start=True,
                              stop=True).then_inc(s16_spread, 1)

            def contract_tile(c, item, n):
                if item == 0 and c > 0:
                    pe.wait_ge(z0_added, n(1, c + 1))
                pe.wait_ge(lo_ready, n(TILES0, TILES0 * c + item + 1))
                pe.matmul(acc0[:], f0l[:, item], hi[:, item], start=item == 0, stop=False)
                pe.matmul(acc0[:], f0h[:, item], lo[:, item], start=False, stop=False)
                pe.matmul(acc0[:], f0h[:, item], hi[:, item], start=False, stop=False)

            def contract_16(c):
                pe.wait_ge(x16_ready, c + 1)
                pe.matmul(acc0[:], f16[:], x16[:], start=False, stop=True).then_inc(acc0_done, 1)

            def fill(c, i, n):
                h, d = BANK1[i]
                at = PLACE[1, c, i]
                if i == 0:
                    pe.wait_ge(c0l_ready, n(1, c + 1))
                wait_bank(at, n)
                out = ring[:, at % RING]
                ch, cl = c0h[:, c % 2, d * P:(d + 1) * P], c0l[:, c % 2, d * P:(d + 1) * P]
                pe.matmul(out, ch, f1l[:, h:h + HPB], start=True, stop=False)
                pe.matmul(out, ch, f1h[:, h:h + HPB], start=False, stop=False)
                pe.matmul(out, cl, f1h[:, h:h + HPB], start=False, stop=True).then_inc(filled, 1)

            def turn(c):
                pe.wait_ge(staged, c + 1)
                if not (isinstance(c, int) and c == 0):
                    pe.wait_ge(p16_ready, c)
                for d in range(DPC):
                    src = stage[:, d].rearrange("p r x -> p (r x)")
                    t = pe.transpose(misc[:, d * P:(d + 1) * P], src, ident[:])
                t.then_inc(turned, 1)

            def turn_z1(half):
                pe.wait_ge(z1_ready, 3 if half else 1)
                if half:
                    pe.wait_ge(zsum_ready, 1)
                for g in range(GROUPS // 2):
                    t = pe.transpose(misc[:, g * P:(g + 1) * P],
                                     z1_rows[:, half * GROUPS // 2 + g], ident[:])
                t.then_inc(z1_turned, 1)

            def iteration(k, base=None):
                def n(rate, const):
                    return const if base is None else base * (rate * 4) + const
                for i in range(BANKS1):
                    for item in range(TILES0):
                        if i == PE_AT[item] and k < LAST:
                            spread_tile(k + 1, item, n)
                    fill(k, i, n)
                    for item in range(TILES0):
                        if i == PE_TILE[item] and k < LAST:
                            contract_tile(k + 1, item, n)
                    if i == PE_16 and k < LAST:
                        contract_16(n(1, k + 1))
                    if i == PE_TURN and k + 2 < CHUNKS:
                        turn(n(1, k + 2))
                    if i == TAIL_PE and k == LAST:
                        turn_z1(0)

            def static(rate, const):
                return const

            pe.wait_ge(const_in, 32)
            pe.wait_ge(shift_ready, 1)
            turn(0)
            for item in range(TILES0):
                spread_tile(0, item, static)
            pe.wait_ge(split_hi, 3)
            pe.wait_ge(split_lo, 4)
            for item in range(TILES0):
                contract_tile(0, item, static)
            contract_16(0)
            turn(1)
            iteration(0)
            iteration(1)
            with pe.Fori(0, (CHUNKS - 4) // 4) as i:
                for k in range(2, 6):
                    iteration(k, i)
            iteration(LAST - 1)
            iteration(LAST)

            pe.wait_ge(tower_in, TOWER_IN)
            for half in range(2):
                cols = slice(512 * half, 512 * (half + 1))
                if half:
                    turn_z1(1)
                pe.wait_ge(dense_ready, 2)
                pe.wait_ge(z0_ready, half + 1)
                pe.wait_ge(zsum_ready, half + 1)
                for m in range(H1 // P):
                    ms = slice(m * P, (m + 1) * P)
                    if half:
                        pe.wait_ge(h1_ready, m + 1)
                    else:
                        wait_bank(len(FILLS) + m, static)
                    o = ring[:, m]
                    pe.matmul(o, wt1_sb[:, 0, ms], zsum[:, 0, cols], start=True, stop=False)
                    pe.matmul(o, wt1_sb[:, 1, ms], zsum[:, 1, cols], start=False, stop=False)
                    pe.matmul(o, wt1d_r[:, ms], dense_r[:, cols], start=False,
                              stop=True).then_inc(h1_sum, 1)
                for m in range(H2 // P):
                    if half:
                        pe.wait_ge(h2_ready, m + 1)
                    else:
                        wait_bank(len(FILLS) + H1 // P + m, static)
                    for t in range(H1 // P):
                        if m == 0:
                            pe.wait_ge(h1_ready, 4 * half + t + 1)
                        mm = pe.matmul(ring[:, H1 // P + m], wt2_sb[:, t, m * P:(m + 1) * P], h1[:, t],
                                       start=(t == 0), stop=(t == H1 // P - 1))
                    mm.then_inc(h2_sum, 1)
                if half:
                    pe.wait_ge(y_ready, 1)
                for t in range(H2 // P):
                    pe.wait_ge(h2_ready, 2 * half + t + 1)
                    mm = pe.matmul(acc0[0:1, :], wt3_sb[:, t:t + 1], h2[:, t],
                                   start=(t == 0), stop=(t == H2 // P - 1))
                mm.then_inc(y_sum, 1)


def layout_constants():
    k, col = np.arange(P), np.arange(P)
    takes = [(col % F + 4 * t + col // F) % F for t in range(TILES0)]
    takes.append((col % F + 16) % F)
    out = np.zeros((P, 6 * P), np.float32)
    for t, f in enumerate(takes):
        out[:, t * P:(t + 1) * P] = (k[:, None] % F == f[None, :]) & (k[:, None] < 2 * F)
    out[:, 5 * P:] = np.eye(P)
    return out


def kernel(**inputs):
    import concourse.bacc as bacc
    from concourse.bass_utils import run_bass_kernel_spmd

    x = {k: np.asarray(v) for k, v in inputs.items()}
    f0 = x["L0_rec_filter_0"][0].reshape(F, F, N)
    f = np.arange(F)
    w0a = np.zeros((P, 5, N), np.float32)
    w0b = np.zeros((P, 4, N), np.float32)
    for s in range(16):
        r = slice((s % 4) * F, (s % 4 + 1) * F)
        w0a[r, s // 4] = f0[f, (f + s) % F]
        if s:
            w0b[r, s // 4] = f0[(f + s) % F, f]
    for r in range(4):
        w0a[r * F:(r + 1) * F, 4] = f0[f, (f + 16) % F]
    w1 = x["L0_rec_filter_1"][0].reshape(F, N, N).transpose(1, 0, 2)
    dense_t, wt1d = np.zeros((P, B), np.float32), np.zeros((P, H1), np.float32)
    for r in (0, 32, 64):
        dense_t[r:r + DENSE], wt1d[r:r + DENSE] = x["dense_ctx"].T, x["W_top1"][2 * N:]
    arrays = {f"tbl_{i}": x[f"tbl_{i}"] for i in range(F)}
    arrays |= {
        "ids": x["ids"], "w0a": w0a, "w0b": w0b, "w1": w1, "consts": layout_constants(),
        "dense_t": dense_t,
        "wt1": x["W_top1"][:2 * N], "wt1d": wt1d, "wt2": x["W_top2"],
        "wt3": np.ascontiguousarray(x["W_top3"].reshape(H2 // P, P).T),
        "bt1": np.ascontiguousarray(x["b_top1"].reshape(H1 // P, P).T),
        "bt2": np.ascontiguousarray(x["b_top2"].reshape(H2 // P, P).T),
    }
    arrays = {f"in_{k}": np.ascontiguousarray(v) for k, v in arrays.items()}
    nc = bacc.Bacc("TRN2", target_bir_lowering=False, num_devices=1)
    ap = {k: nc.dram_tensor(k, v.shape, mybir.dt.from_np(v.dtype), kind="ExternalInput").ap()
          for k, v in arrays.items()}
    out = nc.dram_tensor("out", (B,), F32, kind="ExternalOutput").ap()
    build(nc, [ap[f"in_tbl_{i}"] for i in range(F)], ap["in_ids"], ap["in_w0a"], ap["in_w0b"],
          ap["in_w1"], ap["in_consts"], ap["in_dense_t"], ap["in_wt1"], ap["in_wt1d"], ap["in_wt2"],
          ap["in_wt3"], ap["in_bt1"], ap["in_bt2"], out)
    r = run_bass_kernel_spmd(nc, [arrays], core_ids=[0])
    return r.results[0]["out"].reshape(B, 1)
```
